# Optimizing a Trainium2 kernel written in Bass

```python
import numpy as np
import jax
import jax.numpy as jnp

def _softmax(x, axis=-1):
    return jax.nn.softmax(x, axis=axis)

def _gelu(x):
    return jax.nn.gelu(x, approximate=True)

def _silu(x):
    return jax.nn.silu(x)

def _sigmoid(x):
    return jax.nn.sigmoid(x)

def _layernorm(x, axis=-1, eps=1e-05):
    m = jnp.mean(x, axis=axis, keepdims=True)
    v = jnp.var(x, axis=axis, keepdims=True)
    return (x - m) / jnp.sqrt(v + eps)

def _scatter_add(tgt, idx, src, axis=0):
    return tgt.at[idx].add(src)

def _segment_sum(src, seg, n):
    return jax.ops.segment_sum(src, seg, n)
kernel_name = 'mk_gnn_preln_d4_gnn_r32_cd8cd6'

def setup_inputs(seed: int=0):
    np.random.seed(seed)
    _w = jnp.asarray

    def _rec_inputs():
        import jax
        import jax.numpy as jnp
        _gk = jax.random.key(seed)
        x = -0.000202 + 1 * jax.random.normal(jax.random.fold_in(_gk, 1), (3125, 128), jnp.float32)
        src = jax.random.randint(jax.random.fold_in(_gk, 2), (100000,), 0, 3125, jnp.int32)
        dst = jax.random.randint(jax.random.fold_in(_gk, 3), (100000,), 0, 3125, jnp.int32)
        _o = jnp.argsort(dst, stable=True)
        src = src[_o]
        dst = dst[_o]
        edge_attr_16 = -1.02531e-05 + 0.999808 * jax.random.normal(jax.random.fold_in(_gk, 12), (100000, 16), jnp.float32)
        edge_attr_3 = 0.000844983 + 0.999762 * jax.random.normal(jax.random.fold_in(_gk, 13), (100000, 3), jnp.float32)
        return (x, src, dst, edge_attr_16, edge_attr_3)
    x, src, dst, edge_attr_16, edge_attr_3 = _rec_inputs()

    def _L0_gnn_setup():
        import jax, jax.numpy as jnp
        import numpy as np
        N_NODES = 50000
        N_EDGES = 20000
        HIDDEN = 128
        EDGE_DIM = 3

        def _glorot(key, shape):
            fan_in, fan_out = (shape[0], shape[1])
            lim = (6.0 / (fan_in + fan_out)) ** 0.5
            return jax.random.uniform(key, shape, jnp.float32, -lim, lim)
        key = jax.random.key(seed)
        ks = jax.random.split(key, 12)
        x = jax.random.normal(ks[0], (N_NODES, HIDDEN), jnp.float32)
        edge_index = jax.random.randint(ks[1], (2, N_EDGES), 0, N_NODES, jnp.int64)
        edge_attr = jax.random.normal(ks[2], (N_EDGES, EDGE_DIM), jnp.float32)
        params = {'W_msg1': _glorot(ks[3], (2 * HIDDEN + EDGE_DIM, HIDDEN)), 'b_msg1': jnp.zeros((HIDDEN,), jnp.float32), 'W_msg2': _glorot(ks[4], (HIDDEN, HIDDEN)), 'b_msg2': jnp.zeros((HIDDEN,), jnp.float32), 'W_gate': _glorot(ks[5], (2 * HIDDEN, HIDDEN)), 'b_gate': jnp.zeros((HIDDEN,), jnp.float32), 'W_upd1': _glorot(ks[6], (2 * HIDDEN, HIDDEN)), 'b_upd1': jnp.zeros((HIDDEN,), jnp.float32), 'W_upd2': _glorot(ks[7], (HIDDEN, HIDDEN)), 'b_upd2': jnp.zeros((HIDDEN,), jnp.float32), 'ln_gamma': jnp.ones((HIDDEN,), jnp.float32), 'ln_beta': jnp.zeros((HIDDEN,), jnp.float32)}
        return dict(x=x, edge_index=edge_index, edge_attr=edge_attr, **params)
    _L0_gnn_all = _L0_gnn_setup()
    _L0_gnn_in = {k: v for k, v in _L0_gnn_all.items() if k in ('W_msg1', 'b_msg1', 'W_msg2', 'b_msg2', 'W_gate', 'b_gate', 'W_upd1', 'b_upd1', 'W_upd2', 'b_upd2', 'ln_gamma', 'ln_beta')}
    del _L0_gnn_all

    def _L1_gnn_setup():
        import jax, jax.numpy as jnp
        import numpy as np
        N = 50000
        E = 18750
        D = 128
        FE = 16
        L = 5

        def _sage_conv(x, edge_attr, src, dst, W, b, ew, eb):
            n = x.shape[0]
            edge_emb = edge_attr @ ew.T + eb
            msg = x[src] + edge_emb
            agg = jax.ops.segment_sum(msg, dst, num_segments=n)
            agg = agg + x + eb
            deg = jax.ops.segment_sum(jnp.ones((src.shape[0],), x.dtype), dst, num_segments=n) + 1.0
            mean = agg / deg[:, None]
            return mean @ W + b
        key = jax.random.key(seed)
        ks = jax.random.split(key, 6)
        x = jax.random.normal(ks[0], (N, D), dtype=jnp.float32)
        edge_attr = jax.random.normal(ks[1], (E, FE), dtype=jnp.float32)
        src = jax.random.randint(ks[2], (E,), 0, N, dtype=jnp.int32)
        dst = (src + 1 + jax.random.randint(ks[3], (E,), 0, N - 1, dtype=jnp.int32)) % N
        g = float(np.sqrt(6.0 / (D + D)))
        Ws = jax.random.uniform(ks[4], (L, D, D), jnp.float32, -g, g)
        bs = jnp.zeros((L, D), jnp.float32)
        ge = float(np.sqrt(6.0 / (D + FE)))
        ews = jax.random.uniform(ks[5], (L, D, FE), jnp.float32, -ge, ge)
        ebs = jnp.zeros((L, D), jnp.float32)
        return {'x': x, 'edge_attr': edge_attr, 'src': src, 'dst': dst, 'Ws': Ws, 'bs': bs, 'ews': ews, 'ebs': ebs}
    _L1_gnn_all = _L1_gnn_setup()
    _L1_gnn_in = {k: v for k, v in _L1_gnn_all.items() if k in ('Ws', 'bs', 'ews', 'ebs')}
    del _L1_gnn_all

    def _L2_gnn_setup():
        import jax, jax.numpy as jnp
        import numpy as np
        N_NODES = 50000
        N_EDGES = 25000
        IN_C = 128
        HID_C = 2 * IN_C
        OUT_C = 128
        NEG_SLOPE = 0.2

        def _gat_layer(x, edge_src, edge_dst, W, a_src, a_dst, b, n_nodes):
            h = x @ W
            alpha_src = h @ a_src
            alpha_dst = h @ a_dst
            e = alpha_src[edge_src] + alpha_dst[edge_dst]
            e = jnp.where(e > 0, e, NEG_SLOPE * e)
            m = jax.ops.segment_max(e, edge_dst, num_segments=n_nodes)
            w = jnp.exp(e - m[edge_dst])
            z = jax.ops.segment_sum(w, edge_dst, num_segments=n_nodes)
            alpha = w / z[edge_dst]
            out = jax.ops.segment_sum(alpha[:, None] * h[edge_src], edge_dst, num_segments=n_nodes)
            return out + b
        key = jax.random.key(seed)
        ks = jax.random.split(key, 12)
        x = jax.random.normal(ks[0], (N_NODES, IN_C), dtype=jnp.float32)
        edge_index = jax.random.randint(ks[1], (2, N_EDGES), 0, N_NODES, dtype=jnp.int32)

        def glorot(k, shape):
            fan_in = shape[0] if len(shape) == 2 else shape[0]
            return jax.random.normal(k, shape, dtype=jnp.float32) / np.sqrt(fan_in)
        W1 = glorot(ks[2], (IN_C, HID_C))
        a1_src = glorot(ks[3], (HID_C,))
        a1_dst = glorot(ks[4], (HID_C,))
        b1 = jnp.zeros((HID_C,), dtype=jnp.float32)
        W2 = glorot(ks[5], (HID_C, OUT_C))
        a2_src = glorot(ks[6], (OUT_C,))
        a2_dst = glorot(ks[7], (OUT_C,))
        b2 = jnp.zeros((OUT_C,), dtype=jnp.float32)
        return {'x': x, 'edge_index': edge_index, 'W1': W1, 'a1_src': a1_src, 'a1_dst': a1_dst, 'b1': b1, 'W2': W2, 'a2_src': a2_src, 'a2_dst': a2_dst, 'b2': b2}
    _L2_gnn_all = _L2_gnn_setup()
    _L2_gnn_in = {k: v for k, v in _L2_gnn_all.items() if k in ('W1', 'a1_src', 'a1_dst', 'b1', 'W2', 'a2_src', 'a2_dst', 'b2')}
    del _L2_gnn_all

    def _L3_gnn_setup():
        import jax, jax.numpy as jnp
        from jax import lax
        import numpy as np
        N_NODES = 50000
        N_EDGES = 25000
        IN_CH = 128
        HEADS = 4
        OUT_CH = 32
        TOP_K = 8

        def _topk_mask_1h(e_h, row, k):
            E = e_h.shape[0]
            order = jnp.lexsort((-e_h, row))
            srow = row[order]
            seg_start = jnp.searchsorted(srow, srow, side='left')
            pos_in_seg = jnp.arange(E, dtype=seg_start.dtype) - seg_start
            keep_sorted = pos_in_seg < k
            return jnp.zeros((E,), jnp.bool_).at[order].set(keep_sorted)
        key = jax.random.key(seed)
        k1, k2, k3, k4 = jax.random.split(key, 4)
        x = jax.random.normal(k1, (N_NODES, IN_CH), jnp.float32)
        edge_index = jax.random.randint(k2, (2, N_EDGES), 0, N_NODES, dtype=jnp.int32)
        scale = float(np.sqrt(2.0 / (IN_CH + HEADS * OUT_CH)))
        W = jax.random.normal(k3, (IN_CH, HEADS * OUT_CH), jnp.float32) * scale
        att = jax.random.normal(k4, (HEADS, 2 * OUT_CH), jnp.float32) * 0.1
        return {'x': x, 'W': W, 'att': att, 'edge_index': edge_index}
    _L3_gnn_all = _L3_gnn_setup()
    _L3_gnn_in = {k: v for k, v in _L3_gnn_all.items() if k in ('W', 'att')}
    del _L3_gnn_all
    return {'x': x, 'src': src, 'dst': dst, 'edge_attr_16': edge_attr_16, 'edge_attr_3': edge_attr_3, 'L0_gnn_W_msg1': _L0_gnn_in['W_msg1'], 'L0_gnn_b_msg1': _L0_gnn_in['b_msg1'], 'L0_gnn_W_msg2': _L0_gnn_in['W_msg2'], 'L0_gnn_b_msg2': _L0_gnn_in['b_msg2'], 'L0_gnn_W_gate': _L0_gnn_in['W_gate'], 'L0_gnn_b_gate': _L0_gnn_in['b_gate'], 'L0_gnn_W_upd1': _L0_gnn_in['W_upd1'], 'L0_gnn_b_upd1': _L0_gnn_in['b_upd1'], 'L0_gnn_W_upd2': _L0_gnn_in['W_upd2'], 'L0_gnn_b_upd2': _L0_gnn_in['b_upd2'], 'L0_gnn_ln_gamma': _L0_gnn_in['ln_gamma'], 'L0_gnn_ln_beta': _L0_gnn_in['ln_beta'], 'L1_gnn_Ws': _L1_gnn_in['Ws'], 'L1_gnn_bs': _L1_gnn_in['bs'], 'L1_gnn_ews': _L1_gnn_in['ews'], 'L1_gnn_ebs': _L1_gnn_in['ebs'], 'L2_gnn_W1': _L2_gnn_in['W1'], 'L2_gnn_a1_src': _L2_gnn_in['a1_src'], 'L2_gnn_a1_dst': _L2_gnn_in['a1_dst'], 'L2_gnn_b1': _L2_gnn_in['b1'], 'L2_gnn_W2': _L2_gnn_in['W2'], 'L2_gnn_a2_src': _L2_gnn_in['a2_src'], 'L2_gnn_a2_dst': _L2_gnn_in['a2_dst'], 'L2_gnn_b2': _L2_gnn_in['b2'], 'L3_gnn_W': _L3_gnn_in['W'], 'L3_gnn_att': _L3_gnn_in['att']}

def reference(x, src, dst, edge_attr_16, edge_attr_3, L0_gnn_W_msg1, L0_gnn_b_msg1, L0_gnn_W_msg2, L0_gnn_b_msg2, L0_gnn_W_gate, L0_gnn_b_gate, L0_gnn_W_upd1, L0_gnn_b_upd1, L0_gnn_W_upd2, L0_gnn_b_upd2, L0_gnn_ln_gamma, L0_gnn_ln_beta, L1_gnn_Ws, L1_gnn_bs, L1_gnn_ews, L1_gnn_ebs, L2_gnn_W1, L2_gnn_a1_src, L2_gnn_a1_dst, L2_gnn_b1, L2_gnn_W2, L2_gnn_a2_src, L2_gnn_a2_dst, L2_gnn_b2, L3_gnn_W, L3_gnn_att):
    import jax
    import jax.numpy as jnp

    def _L0_gnn_ref(x, edge_index, edge_attr, W_msg1, b_msg1, W_msg2, b_msg2, W_gate, b_gate, W_upd1, b_upd1, W_upd2, b_upd2, ln_gamma, ln_beta):
        import jax, jax.numpy as jnp
        import numpy as np
        N_NODES = 50000
        N_EDGES = 20000
        HIDDEN = 128
        EDGE_DIM = 3

        def _glorot(key, shape):
            fan_in, fan_out = (shape[0], shape[1])
            lim = (6.0 / (fan_in + fan_out)) ** 0.5
            return jax.random.uniform(key, shape, jnp.float32, -lim, lim)
        src, dst = (edge_index[0], edge_index[1])
        source = x[src]
        target = x[dst]
        msg_in = jnp.concatenate([source, target, edge_attr], axis=-1)
        h = jax.nn.relu(msg_in @ W_msg1 + b_msg1)
        messages = h @ W_msg2 + b_msg2
        aggregated = jax.ops.segment_sum(messages, dst, num_segments=x.shape[0])
        upd_in = jnp.concatenate([x, aggregated], axis=-1)
        gate = jax.nn.sigmoid(upd_in @ W_gate + b_gate)
        update = jax.nn.relu(upd_in @ W_upd1 + b_upd1) @ W_upd2 + b_upd2
        out = gate * update + (1.0 - gate) * x
        mu = jnp.mean(out, axis=-1, keepdims=True)
        var = jnp.var(out, axis=-1, keepdims=True)
        normed = (out - mu) * jax.lax.rsqrt(var + 1e-05)
        return normed * ln_gamma + ln_beta

    def _L1_gnn_ref(x, edge_attr, src, dst, Ws, bs, ews, ebs):
        import jax, jax.numpy as jnp
        import numpy as np
        N = 50000
        E = 18750
        D = 128
        FE = 16
        L = 5

        def _sage_conv(x, edge_attr, src, dst, W, b, ew, eb):
            n = x.shape[0]
            edge_emb = edge_attr @ ew.T + eb
            msg = x[src] + edge_emb
            agg = jax.ops.segment_sum(msg, dst, num_segments=n)
            agg = agg + x + eb
            deg = jax.ops.segment_sum(jnp.ones((src.shape[0],), x.dtype), dst, num_segments=n) + 1.0
            mean = agg / deg[:, None]
            return mean @ W + b
        h = x
        for l in range(L):
            h = _sage_conv(h, edge_attr, src, dst, Ws[l], bs[l], ews[l], ebs[l])
            if l < L - 1:
                h = jax.nn.relu(h)
        return h

    def _L2_gnn_ref(x, edge_index, W1, a1_src, a1_dst, b1, W2, a2_src, a2_dst, b2):
        import jax, jax.numpy as jnp
        import numpy as np
        N_NODES = 50000
        N_EDGES = 25000
        IN_C = 128
        HID_C = 2 * IN_C
        OUT_C = 128
        NEG_SLOPE = 0.2

        def _gat_layer(x, edge_src, edge_dst, W, a_src, a_dst, b, n_nodes):
            h = x @ W
            alpha_src = h @ a_src
            alpha_dst = h @ a_dst
            e = alpha_src[edge_src] + alpha_dst[edge_dst]
            e = jnp.where(e > 0, e, NEG_SLOPE * e)
            m = jax.ops.segment_max(e, edge_dst, num_segments=n_nodes)
            w = jnp.exp(e - m[edge_dst])
            z = jax.ops.segment_sum(w, edge_dst, num_segments=n_nodes)
            alpha = w / z[edge_dst]
            out = jax.ops.segment_sum(alpha[:, None] * h[edge_src], edge_dst, num_segments=n_nodes)
            return out + b
        n = x.shape[0]
        loops = jnp.arange(n, dtype=edge_index.dtype)
        src = jnp.concatenate([edge_index[0], loops])
        dst = jnp.concatenate([edge_index[1], loops])
        h = _gat_layer(x, src, dst, W1, a1_src, a1_dst, b1, n)
        h = jax.nn.relu(h)
        out = _gat_layer(h, src, dst, W2, a2_src, a2_dst, b2, n)
        return out

    def _L3_gnn_ref(x, W, att, edge_index):
        import jax, jax.numpy as jnp
        from jax import lax
        import numpy as np
        N_NODES = 50000
        N_EDGES = 25000
        IN_CH = 128
        HEADS = 4
        OUT_CH = 32
        TOP_K = 8

        def _topk_mask_1h(e_h, row, k):
            E = e_h.shape[0]
            order = jnp.lexsort((-e_h, row))
            srow = row[order]
            seg_start = jnp.searchsorted(srow, srow, side='left')
            pos_in_seg = jnp.arange(E, dtype=seg_start.dtype) - seg_start
            keep_sorted = pos_in_seg < k
            return jnp.zeros((E,), jnp.bool_).at[order].set(keep_sorted)
        N = x.shape[0]
        H, C = (HEADS, OUT_CH)
        h = (x @ W).reshape(N, H, C)
        loops = jnp.arange(N, dtype=edge_index.dtype)
        ei = jnp.concatenate([edge_index, jnp.stack([loops, loops])], axis=1)
        row, col = (ei[0], ei[1])
        x_i = h[row]
        x_j = h[col]
        a_i, a_j = (att[:, :C], att[:, C:])
        e = jnp.einsum('ehc,hc->eh', x_i, a_i) + jnp.einsum('ehc,hc->eh', x_j, a_j)
        e = jax.nn.leaky_relu(e, negative_slope=0.2)
        mask = jax.vmap(lambda eh: _topk_mask_1h(eh, row, TOP_K), in_axes=1, out_axes=1)(e)
        e = jnp.where(mask, e, -jnp.inf)
        seg_max = jax.ops.segment_max(e, row, num_segments=N)
        ez = jnp.exp(e - lax.stop_gradient(seg_max)[row])
        denom = jax.ops.segment_sum(ez, row, num_segments=N)
        alpha = ez / denom[row]
        out = jax.ops.segment_sum(alpha[:, :, None] * x_j, row, num_segments=N)
        out = out.reshape(N, H * C)
        return jax.nn.elu(out)
    edge_index = jnp.stack([src, dst])
    h = jnp.maximum(_layernorm(x, axis=-1), 0.0)
    x = x + _L0_gnn_ref(h, edge_index, edge_attr_3, L0_gnn_W_msg1, L0_gnn_b_msg1, L0_gnn_W_msg2, L0_gnn_b_msg2, L0_gnn_W_gate, L0_gnn_b_gate, L0_gnn_W_upd1, L0_gnn_b_upd1, L0_gnn_W_upd2, L0_gnn_b_upd2, L0_gnn_ln_gamma, L0_gnn_ln_beta)
    h = jnp.maximum(_layernorm(x, axis=-1), 0.0)
    x = x + _L1_gnn_ref(h, edge_attr_16, src, dst, L1_gnn_Ws, L1_gnn_bs, L1_gnn_ews, L1_gnn_ebs)
    h = jnp.maximum(_layernorm(x, axis=-1), 0.0)
    x = x + _L2_gnn_ref(h, edge_index, L2_gnn_W1, L2_gnn_a1_src, L2_gnn_a1_dst, L2_gnn_b1, L2_gnn_W2, L2_gnn_a2_src, L2_gnn_a2_dst, L2_gnn_b2)
    h = jnp.maximum(_layernorm(x, axis=-1), 0.0)
    x = x + _L3_gnn_ref(h, L3_gnn_W, L3_gnn_att, edge_index)
    return x

_drawn_inputs = setup_inputs


def setup_inputs(seed=0):
    import zlib

    import numpy as np

    out = dict(_drawn_inputs(seed))
    spreads = {'L0_gnn_b_msg1': (0.0, 0.1),
     'L0_gnn_b_msg2': (0.0, 0.1),
     'L0_gnn_b_gate': (0.0, 0.8),
     'L0_gnn_b_upd1': (0.0, 0.8),
     'L0_gnn_b_upd2': (0.0, 0.7),
     'L0_gnn_ln_gamma': (1.0, 0.2),
     'L0_gnn_ln_beta': (0.0, 0.1),
     'L1_gnn_bs': (0.0, 0.1),
     'L1_gnn_ebs': (0.0, 0.1),
     'L2_gnn_b1': (0.0, 0.1),
     'L2_gnn_b2': (0.0, 0.1)}
    factors = {'L2_gnn_a1_src': 3.902, 'L2_gnn_a1_dst': 8.0, 'L2_gnn_a2_src': 8.0, 'L2_gnn_a2_dst': 8.0}
    for name, (base, spread) in spreads.items():
        noise = np.random.default_rng([zlib.crc32(name.encode()), seed]).standard_normal(out[name].shape)
        drawn = base * np.exp(spread * noise) if base else spread * noise
        out[name] = jnp.asarray(drawn.astype(out[name].dtype))
    for name, factor in factors.items():
        out[name] = (out[name] * factor).astype(out[name].dtype)
    return out
```

```python
import concourse.bass as bass
from concourse import mybir
from contextlib import ExitStack

N, D, E = 3125, 128, 100000
P = 125
NT = N // P
CE = 1000
ET = CE // P
NC = E // CE
STEPS = NC + NT - 1
H0, H1 = 1563, 1562
QW = 391
EXT = 1 + 16 + 1
MW = 1 + 16 + D
EPS = 1e-5
HEADS, HC, TOP = 4, 32, 8
RW = HC + 1
ABSENT = -60000.0

F32, F16, BF16, I32 = mybir.dt.float32, mybir.dt.float16, mybir.dt.bfloat16, mybir.dt.int32
ALU = mybir.AluOpType
ACT = mybir.ActivationFunctionType
AX = mybir.AxisListType
RMAX = bass.bass_isa.ReduceOp.max


class Serial:

    def __init__(self, eng, sem, base=0):
        self.eng, self.sem, self.base, self.n = eng, sem, base, 0

    def __call__(self, ins):
        self.n += 1
        ins.then_inc(self.sem, 1)
        self.eng.wait_ge(self.sem, self.base + self.n)


def rows(ap):
    return ap.rearrange("(i p) f -> p i f", p=P)


def bcast(ap, n, m):
    return ap.unsqueeze(2).broadcast_to([ap.shape[0], n, m])


class Norm:

    def __init__(self, nc, ctx, name, xc=None):
        self.nc, self.name = nc, name
        self.st = ctx.enter_context(nc.sbuf_tensor(f"{name}_stats", [P, 4, NT], F32))
        self.sq = ctx.enter_context(nc.sbuf_tensor(f"{name}_square", [P, NT, D], F32))
        self.var_ready = ctx.enter_context(nc.semaphore(f"{name}_var_ready"))
        self.std_ready = ctx.enter_context(nc.semaphore(f"{name}_std_ready"))

    def vector(self, dve, link, out, x):
        nc, st = self.nc, self.st
        link(nc.vector.tensor_reduce(st[:, 0, :], x, AX.X, ALU.add))
        link(nc.vector.tensor_scalar(st[:, 1, :], st[:, 0, :], 1.0 / D, None, ALU.mult))
        link(nc.vector.tensor_tensor(out, x, bcast(st[:, 1, :], NT, D), ALU.subtract))
        link(nc.vector.tensor_tensor(self.sq[:], out, out, ALU.mult))
        link(nc.vector.tensor_reduce(st[:, 2, :], self.sq[:], AX.X, ALU.add))
        nc.vector.tensor_scalar(st[:, 3, :], st[:, 2, :], 1.0 / D, EPS, ALU.mult, ALU.add).then_inc(self.var_ready, 1)
        dve.wait_ge(self.std_ready, 1)
        link(nc.vector.reciprocal(st[:, 1, :], st[:, 0, :]))
        link(nc.vector.tensor_tensor(out, out, bcast(st[:, 1, :], NT, D), ALU.mult))

    def scalar(self, act):
        act.wait_ge(self.var_ready, 1)
        self.nc.scalar.activation(self.st[:, 0, :], self.st[:, 3, :], ACT.Sqrt).then_inc(self.std_ready, 1)


def prepare(nc, t, a, keep):
    with ExitStack() as ctx:
        sb = lambda n, s, d: ctx.enter_context(nc.sbuf_tensor(n, s, d))
        pb = lambda n, s, d: ctx.enter_context(nc.psum_tensor(n, s, d))
        sem = lambda n: ctx.enter_context(nc.semaphore(n))
        x, h = keep["x"], keep["h"]
        hT = sb("A_hT", [D, 2, P], F32)
        w = sb("A_w", [D, 2, D], F32)
        b1 = sb("A_b1", [P, D], F32)
        pq = sb("A_pq", [P, 2, NT, D], F32)
        last_dst, last_f = sb("last_dst", [NC - 1, ET], I32), sb("last_f", [NC - 1, 1], F32)
        edges_of = sb("edges_of", [NC - 1, NT - 1], F32)
        hit = sb("hit", [NC - 1, NT - 1], F32)
        chunk_id, leave, window_of = sb("chunk_id", [NC - 1, 1], F32), sb("leave", [NC - 1, 1], F32), sb("last_window", [NC - 1, 1], F32)
        step_id = sb("step_id", [P, STEPS], F32)
        left = sb("left", [NC - 1, STEPS], F32)
        ones = sb("A_ones", [NC - 1, P], F32)
        tab = sb("tab", [P, 2, STEPS], F32)
        psT = pb("A_psT", [D, 2, 512], F32)
        psP = pb("A_psP", [P, 2, 512], F32)
        psQ = pb("A_psQ", [P, 2, 512], F32)
        psC = pb("A_psC", [P, STEPS], F32)
        loads, wloads, iotas, chain, hready = (sem(n) for n in ("A_loads", "A_wloads", "A_iotas", "A_chain", "A_hready"))
        hT_ps, hT_ready, pq_ps, p_out, q_out, cmp_ready, cnt_ready, stored = (
            sem(n) for n in ("A_hT_ps", "A_hT_ready", "A_pq_ps", "A_p_out", "A_q_out", "A_cmp", "A_cnt", "A_stored"))
        norm = Norm(nc, ctx, "A_norm")
        block = ctx.enter_context(nc.Block())

        @block.sync
        def _(sp):
            sp.dma_start(x[:], rows(a["x"])).then_inc(loads, 16)
            sp.dma_start(w[:], a["W_msg1"][0:2 * D, :].rearrange("(k p) n -> p k n", p=D)).then_inc(wloads, 16)
            sp.dma_start(last_dst[:], a["dst"].rearrange("(c e) -> c e", e=CE)[0:NC - 1, CE - ET:CE]).then_inc(wloads, 16)
            sp.dma_start(b1[:], a["b_msg1"].partition_broadcast(P)).then_inc(wloads, 16)
            sp.wait_ge(p_out, NT)
            sp.dma_start(rows(t["P"]), pq[:, 0, :, :]).then_inc(stored, 16)
            sp.wait_ge(q_out, NT)
            sp.dma_start(rows(t["Q"]), pq[:, 1, :, :]).then_inc(stored, 16)
            sp.wait_ge(stored, 32)

        @block.gpsimd
        def _(pool):
            i = nc.gpsimd.iota
            kw = dict(allow_small_or_imprecise_dtypes=True)
            i(keep["iota_s"][:, :], pattern=[[1, N]], base=-(N // 2), channel_multiplier=0, **kw).then_inc(iotas, 1)
            i(keep["iota_d"][:, :], pattern=[[1, 128]], base=0, channel_multiplier=0, **kw).then_inc(iotas, 1)
            i(edges_of[:, :], pattern=[[P, NT - 1]], base=P, channel_multiplier=0, **kw).then_inc(iotas, 1)
            i(step_id[:, :], pattern=[[1, STEPS]], base=0, channel_multiplier=0, **kw).then_inc(iotas, 1)
            i(chunk_id[:, :], pattern=[[0, 1]], base=0, channel_multiplier=1, **kw).then_inc(iotas, 1)
            i(keep["rowid"][:, :], pattern=[[0, 1]], base=0, channel_multiplier=1, **kw).then_inc(iotas, 1)

        @block.scalar
        def _(act):
            norm.scalar(act)
            for j in range(NT):
                act.wait_ge(hT_ps, j + 1)
                if j >= 2:
                    act.wait_ge(pq_ps, j - 1)
                nc.scalar.copy(hT[:, j % 2, :], psT[:, j % 2, 0:P]).then_inc(hT_ready, 1)
                act.wait_ge(pq_ps, j + 1)
                nc.scalar.copy(pq[:, 0, j, :], psP[:, j % 2, 0:D]).then_inc(p_out, 1)

        @block.tensor
        def _(pe):
            pe.wait_ge(wloads, 48)
            pe.wait_ge(hready, 1)
            pe.wait_ge(cmp_ready, 1)
            nc.tensor.matmul(psC[:, :], ones[:], left[:], start=True, stop=True).then_inc(cnt_ready, 1)
            for j in range(NT):
                if j >= 2:
                    pe.wait_ge(hT_ready, j - 1)
                nc.tensor.transpose(psT[:, j % 2, 0:P], h[:, j, :], keep["ident32"][:]).then_inc(hT_ps, 1)
                pe.wait_ge(hT_ready, j + 1)
                if j >= 2:
                    pe.wait_ge(p_out, j - 1)
                    pe.wait_ge(q_out, j - 1)
                nc.tensor.matmul(psP[:, j % 2, 0:D], hT[:, j % 2, :], w[:, 0, :], start=True, stop=True)
                nc.tensor.matmul(psQ[:, j % 2, 0:D], hT[:, j % 2, :], w[:, 1, :], start=True, stop=True).then_inc(pq_ps, 1)

        @block.vector
        def _(dve):
            link = Serial(dve, chain)
            dve.wait_ge(loads, 16)
            norm.vector(dve, link, h[:], x[:])
            nc.vector.tensor_scalar(h[:], h[:], 0.0, None, ALU.max).then_inc(hready, 1)
            dve.wait_ge(iotas, 6)
            dve.wait_ge(wloads, 48)
            link(nc.vector.tensor_scalar(keep["ident128"][:], keep["iota_d"][:], keep["rowid"][:], None, ALU.is_equal))
            link(nc.vector.tensor_copy(keep["ident32"][:], keep["ident128"][0:P, 0:P]))
            link(nc.vector.tensor_copy(keep["ident16"][:], keep["ident32"][:]))
            link(nc.vector.tensor_copy(last_f[:], last_dst[:, ET - 1:ET]))
            link(nc.vector.tensor_scalar(hit[:], edges_of[:], last_f[:], None, ALU.is_le))
            link(nc.vector.tensor_reduce(window_of[:], hit[:], AX.X, ALU.add))
            link(nc.vector.tensor_tensor(leave[:], window_of[:], chunk_id[:], ALU.add))
            link(nc.vector.memset(ones[:], 1.0))
            nc.vector.tensor_scalar(left[:], step_id[0:NC - 1, :], leave[:], None, ALU.is_gt).then_inc(cmp_ready, 1)
            dve.wait_ge(cnt_ready, 1)
            link(nc.vector.tensor_copy(tab[:, 0, :], psC[:]))
            link(nc.vector.tensor_tensor(tab[:, 1, :], step_id[:], tab[:, 0, :], ALU.subtract))
            link(nc.vector.tensor_copy(keep["chunk_of"][:], tab[0:1, 0, :]))
            link(nc.vector.tensor_copy(keep["window_of"][:], tab[0:1, 1, :]))
            link(nc.vector.tensor_scalar(keep["base"][:], tab[:, 1, :], float(P), None, ALU.mult))
            link(nc.vector.memset(keep["same"][:], 0.0))
            link(nc.vector.tensor_tensor(keep["same"][:, 1:STEPS], tab[:, 1, 1:STEPS], tab[:, 1, 0:STEPS - 1], ALU.is_equal))
            for j in range(NT):
                dve.wait_ge(pq_ps, j + 1)
                nc.vector.tensor_tensor(pq[:, 1, j, :], psQ[:, j % 2, 0:D], b1[:], ALU.add).then_inc(q_out, 1)


def edge_loop(nc, t, a, keep):
    with ExitStack() as ctx:
        sb = lambda n, s, d: ctx.enter_context(nc.sbuf_tensor(n, s, d))
        pb = lambda n, s, d: ctx.enter_context(nc.psum_tensor(n, s, d))
        sem = lambda n: ctx.enter_context(nc.semaphore(n))
        two = lambda n, s, d: [sb(f"{n}{u}", s, d) for u in range(2)]
        src_i, dst_i = two("src_i", [P, ET], I32), two("dst_i", [P, ET], I32)
        attr3, attr16 = two("attr3", [3, ET, P], F32), two("attr16", [P, ET, 16], F32)
        src_f, dst_f = two("src_f", [P, ET], F32), two("dst_f", [P, ET], F32)
        wc = sb("wc", [3, D], F32)
        same16, same32 = two("same16", [P, P], F16), two("same32", [P, P], F32)
        hot_d, hot_d32 = two("hot_d", [P, ET, P], F16), two("hot_d32", [P, ET, P], F32)
        hot_s = two("hot_s", [P, ET, H0], F16)
        pg, qg, msg = two("pg", [P, ET, D], F32), two("qg", [P, ET, D], F32), two("msg", [P, ET, MW], F32)
        adj = two("adj", [P, N], F16)
        gsum = two("gsum", [P, MW], F32)
        psA = pb("psA", [P, 4, 512], F32)
        psE = pb("psE", [P, ET, D], F32)
        psG = pb("psG", [P, 512], F32)
        in_ready = [sem(f"in_ready{u}") for u in range(2)]
        gathered = [sem(f"gathered{u}") for u in range(2)]
        adj_stored = [sem(f"adj_stored{u}") for u in range(2)]
        (wc_ready, primed, dve_chain, in_used, attr_ps, hot_d_ready, hot_s_ready, attr_added, relu_done,
         hot32_ready, adj_ps, adj_out, gsum_ps, gsum_out, go) = (sem(n) for n in (
            "wc_ready", "primed", "dve_chain", "in_used", "attr_ps", "hot_d_ready", "hot_s_ready", "attr_added",
            "relu_done", "hot32_ready", "adj_ps", "adj_out", "gsum_ps", "gsum_out", "gather_go"))
        src_v = a["src"].rearrange("(c p t) -> c p t", p=P, t=ET)
        dst_v = a["dst"].rearrange("(c p t) -> c p t", p=P, t=ET)
        a16_v = a["attr16"].rearrange("(c p t) f -> c p t f", p=P, t=ET)
        block = ctx.enter_context(nc.Block())

        @block.sync
        def _(sp):
            sp.dma_start(wc[:], a["W_msg1"][2 * D:2 * D + 3, :]).then_inc(wc_ready, 16)
            for u in range(2):
                sp.sem_inc(adj_stored[u], 16)
            with sp.Fori(0, STEPS // 2) as i:
                for u in range(2):
                    k = i * 2 + u
                    c = sp.value_load(keep["chunk_of"][0:1, bass.ds(k, 1)], min_val=0, max_val=NC - 1)
                    sp.wait_ge(in_used, k + 1)
                    sp.wait_ge(attr_ps, k + 1)
                    sp.wait_ge(attr_added, k + 1)
                    for o, v in ((src_i, src_v), (dst_i, dst_v)):
                        sp.dma_start(o[u][:], v[bass.ds(c, 1), :, :].squeeze(0)).then_inc(in_ready[u], 16)
                    sp.dma_start(attr16[u][:], a16_v[bass.ds(c, 1), :, :, :].squeeze(0)).then_inc(in_ready[u], 16)
                    sp.dma_start(attr3[u][:], a["attr3"][bass.ds(c, 1), :, :, :].squeeze(0)).then_inc(in_ready[u], 16)

        @block.gpsimd
        def _(pool):
            with pool.Fori(0, STEPS // 2) as i:
                for u in range(2):
                    k = i * 2 + u
                    pool.wait_ge(in_ready[u], i * 64 + 64)
                    pool.wait_ge(relu_done, k + 1)
                    pool.sem_inc(go, 1)
                    for tt in range(ET):
                        for o, tab, idx in ((pg, "P", src_i), (qg, "Q", dst_i)):
                            nc.gpsimd.indirect_dma_start(
                                out=o[u][:, tt, :], out_offset=None, in_=t[tab],
                                in_offset=bass.IndirectOffsetOnAxis(ap=idx[u][:, tt:tt + 1], axis=0),
                            ).then_inc(gathered[u], 16)

        @block.vector
        def _(dve):
            dve.sem_inc(in_used, 2)
            dve.sem_inc(attr_added, 2)
            dve.sem_inc(hot_s_ready, 2)
            for u in range(2):
                nc.vector.memset(adj[u][:], 0.0)
                nc.vector.memset(gsum[u][:], 0.0)
                last = nc.vector.memset(msg[u][:, :, 0:1], 1.0)
            last.then_inc(primed, 1)
            dve.wait_ge(primed, 1)
            with dve.Fori(0, STEPS // 2) as i:
                for u in range(2):
                    k = i * 2 + u
                    link = Serial(dve, dve_chain, k * 2)
                    dve.wait_ge(in_ready[u], i * 64 + 64)
                    dve.wait_ge(gsum_ps, k + 1)
                    dve.wait_ge(hot32_ready, k + 1)
                    dve.wait_ge(hot_s_ready, k * 2 + 2)
                    nc.vector.tensor_scalar(dst_f[u][:], dst_i[u][:], keep["base"][:, bass.ds(k, 1)], None, ALU.subtract)
                    nc.vector.tensor_scalar(same16[u][:], keep["ident16"][:], keep["same"][:, bass.ds(k, 1)], None, ALU.mult)
                    nc.vector.tensor_scalar(same32[u][:], keep["ident32"][:], keep["same"][:, bass.ds(k, 1)], None, ALU.mult)
                    nc.vector.tensor_copy(msg[u][:, :, 1:17], attr16[u][:])
                    link(nc.vector.tensor_scalar(src_f[u][:], src_i[u][:], float(-(N // 2)), None, ALU.add))
                    dve.sem_inc(in_used, 1)
                    for tt in range(ET):
                        last = nc.vector.tensor_scalar(hot_d[u][:, tt, :], keep["iota_d"][0:P, 0:P], dst_f[u][:, tt:tt + 1], None, ALU.is_equal)
                    last.then_inc(hot_d_ready, 1)
                    dve.wait_ge(adj_ps, k * 8 + 4)
                    for tt in range(ET):
                        last = nc.vector.tensor_scalar(hot_s[0][:, tt, 0:H0], keep["iota_s"][:, 0:H0], src_f[u][:, tt:tt + 1], None, ALU.is_equal)
                    last.then_inc(hot_s_ready, 1)
                    dve.wait_ge(gathered[u], i * (2 * ET * 16) + 2 * ET * 16)
                    dve.wait_ge(attr_ps, k + 3)
                    link(nc.vector.tensor_tensor(pg[u][:], pg[u][:], qg[u][:], ALU.add))
                    nc.vector.tensor_tensor(pg[u][:], pg[u][:], psE[:], ALU.add).then_inc(attr_added, 1)
                    dve.wait_ge(adj_ps, k * 8 + 8)
                    for tt in range(ET):
                        last = nc.vector.tensor_scalar(hot_s[1][:, tt, 0:H1], keep["iota_s"][:, H0:N], src_f[u][:, tt:tt + 1], None, ALU.is_equal)
                    last.then_inc(hot_s_ready, 1)

        @block.scalar
        def _(act):
            act.sem_inc(relu_done, 2)
            act.sem_inc(hot32_ready, 2)
            act.sem_inc(adj_out, 4)
            act.sem_inc(gsum_out, 1)
            with act.Fori(0, STEPS // 2) as i:
                for u in range(2):
                    k = i * 2 + u
                    j = act.value_load(keep["window_of"][0:1, bass.ds(k, 1)], min_val=0, max_val=NT - 1)

                    def out(b):
                        act.wait_ge(adj_ps, k * 8 + b + 9)
                        w = min(QW, (H0 if b < 4 else H1) - (b % 4) * QW)
                        at = (b // 4) * H0 + (b % 4) * QW
                        nc.scalar.copy(adj[u][:, at:at + w], psA[:, b % 4, 0:w]).then_inc(adj_out, 1)

                    act.wait_ge(hot_d_ready, k + 1)
                    act.wait_ge(gsum_ps, k + 1)
                    nc.scalar.copy(hot_d32[u][:], hot_d[u][:]).then_inc(hot32_ready, 1)
                    act.wait_ge(adj_stored[u], i * 16 + 16)
                    for b in range(4):
                        out(b)
                    act.wait_ge(attr_added, k + 3)
                    nc.scalar.activation(msg[u][:, :, 17:MW], pg[u][:], ACT.Relu).then_inc(relu_done, 1)
                    for b in range(4, 8):
                        out(b)
                    act.wait_ge(adj_out, k * 8 + 12)
                    act.wait_ge(adj_stored[1 - u], i * 16 + 16 + 16 * u)
                    act.dma_start(t["C"][bass.ds(j * P, P), :], adj[u][:]).then_inc(adj_stored[u], 16)
                    act.wait_ge(gsum_ps, k + 3)
                    act.wait_ge(gsum_out, k + 1)
                    nc.scalar.copy(gsum[u][:], psG[:, 0:MW])
                    nc.scalar.copy(keep["G"][:, bass.ds(j * MW, MW)], psG[:, 0:MW]).then_inc(gsum_out, 1)
            for u in range(2):
                act.wait_ge(adj_stored[u], (STEPS // 2) * 16 + 16)

        @block.tensor
        def _(pe):
            pe.wait_ge(wc_ready, 16)
            pe.wait_ge(primed, 1)
            pe.sem_inc(attr_ps, 2)
            pe.sem_inc(adj_ps, 8)
            pe.sem_inc(gsum_ps, 2)
            with pe.Fori(0, STEPS // 2) as i:
                for u in range(2):
                    k = i * 2 + u
                    pe.wait_ge(in_ready[u], i * 64 + 64)
                    pe.wait_ge(attr_added, k + 2)
                    for tt in range(ET):
                        last = nc.tensor.matmul(psE[:, tt, :], attr3[u][:, tt, :], wc[:], start=True, stop=True)
                    last.then_inc(attr_ps, 1)
                    pe.wait_ge(hot_d_ready, k + 1)
                    for b in range(8):
                        if b % 4 == 0:
                            pe.wait_ge(hot_s_ready, k * 2 + 3 + b // 4)
                        pe.wait_ge(adj_out, k * 8 + b + 1)
                        w = min(QW, (H0 if b < 4 else H1) - (b % 4) * QW)
                        at = (b // 4) * H0 + (b % 4) * QW
                        q = (b % 4) * QW
                        for tt in range(ET):
                            nc.tensor.matmul(psA[:, b % 4, 0:w], hot_d[u][:, tt, :], hot_s[b // 4][:, tt, q:q + w], start=tt == 0, stop=False)
                        nc.tensor.matmul(psA[:, b % 4, 0:w], same16[u][:], adj[1 - u][:, at:at + w], start=False, stop=True).then_inc(adj_ps, 1)
                    pe.wait_ge(relu_done, k + 3)
                    pe.wait_ge(hot32_ready, k + 3)
                    pe.wait_ge(gsum_out, k + 1)
                    for tt in range(ET):
                        nc.tensor.matmul(psG[:, 0:MW], hot_d32[u][:, tt, :], msg[u][:, tt, :], start=tt == 0, stop=False)
                    nc.tensor.matmul(psG[:, 0:MW], same32[u][:], gsum[1 - u][:], start=False, stop=True).then_inc(gsum_ps, 1)


def node_update(nc, t, a, keep):
    with ExitStack() as ctx:
        sb = lambda n, s, d: ctx.enter_context(nc.sbuf_tensor(n, s, d))
        pb = lambda n, s, d: ctx.enter_context(nc.psum_tensor(n, s, d))
        sem = lambda n: ctx.enter_context(nc.semaphore(n))
        x, h = keep["x"], keep["h"]
        GW = 4 * P
        groups = [(g, min(4, NT - g)) for g in range(0, NT, 4)]
        sums = keep["G"][:].rearrange("p (i f) -> p i f", f=MW)
        ext = sb("ext", [P, NT, EXT], F32)
        wm2, wg, wu1, wu2 = sb("wm2", [D, D], F32), sb("wg", [D, 2, D], F32), sb("wu1", [D, 2, D], F32), sb("wu2", [D, D], F32)
        bm2 = sb("bm2", [1, D], F32)
        bg, bu1, bu2 = sb("bg", [D, 1], F32), sb("bu1", [D, 1], F32), sb("bu2", [D, 1], F32)
        gamma, beta = sb("gamma", [P, D], F32), sb("beta", [P, D], F32)
        hT, sT, eT, aT = sb("hT", [D, GW], F32), sb("sT", [D, GW], F32), sb("eT", [EXT, NT * P], F32), sb("aT", [D, GW], F32)
        gate, up, new = sb("gate", [D, GW], F32), sb("up", [D, GW], F32), sb("new", [D, GW], F32)
        o = sb("o", [P, NT, D], F32)
        psH, psS, psX, psA = pb("C_psH", [D, 512], F32), pb("C_psS", [D, 512], F32), pb("C_psX", [EXT, 512], F32), pb("C_psA", [D, 512], F32)
        psG, psU, psV, psO = pb("C_psG", [D, 512], F32), pb("C_psU", [D, 512], F32), pb("C_psV", [D, 512], F32), pb("C_psO", [P, 4, D], F32)
        (loads, ext_ready, turned, hx_out, s_out, agg_ps, agg_out, gate_ps, gate_out, up_out, up_ps, new_ready,
         back_ps, back_out, chain, stored) = (sem("C_" + n) for n in (
            "loads", "ext_ready", "turned", "hx_out", "s_out", "agg_ps", "agg_out", "gate_ps", "gate_out", "up_out",
            "up_ps", "new_ready", "back_ps", "back_out", "chain", "stored"))
        x_ready, h_ready = sem("C_x_ready"), sem("C_h_ready")
        norm1, norm2 = Norm(nc, ctx, "C_norm1"), Norm(nc, ctx, "C_norm2")
        block = ctx.enter_context(nc.Block())

        @block.sync
        def _(sp):
            for o_, v in ((wm2[:], a["W_msg2"]), (wg[:], a["W_gate"].rearrange("(k p) n -> p k n", p=D)),
                          (wu1[:], a["W_upd1"].rearrange("(k p) n -> p k n", p=D)), (wu2[:], a["W_upd2"]),
                          (bm2[:], a["b_msg2"].unsqueeze(0)), (bg[:], a["b_gate"].unsqueeze(1)), (bu1[:], a["b_upd1"].unsqueeze(1)),
                          (bu2[:], a["b_upd2"].unsqueeze(1)), (gamma[:], a["ln_gamma"].partition_broadcast(P)),
                          (beta[:], a["ln_beta"].partition_broadcast(P))):
                sp.dma_start(o_, v, allow_slow_non_contiguous=True).then_inc(loads, 16)
            sp.wait_ge(hx_out, len(groups))
            sp.dma_start(t["ext"], eT[:]).then_inc(stored, 16)
            sp.wait_ge(x_ready, 1)
            sp.dma_start(rows(t["x"]), x[:]).then_inc(stored, 16)
            sp.wait_ge(h_ready, 1)
            sp.dma_start(rows(t["h"]), h[:]).then_inc(stored, 16)
            sp.wait_ge(stored, 48)

        @block.tensor
        def _(pe):
            pe.wait_ge(loads, 160)
            pe.wait_ge(ext_ready, 1)
            for g, (i0, n) in enumerate(groups):
                w = n * P
                if g:
                    pe.wait_ge(hx_out, g)
                    pe.wait_ge(s_out, g)
                for q in range(n):
                    c = slice(q * P, q * P + P)
                    nc.tensor.transpose(psH[:, c], h[:, i0 + q, :], keep["ident32"][:])
                    nc.tensor.transpose(psS[:, c], sums[:, i0 + q, 17:MW], keep["ident32"][:])
                    last = nc.tensor.transpose(psX[:, c], ext[:, i0 + q, :], keep["ident32"][:])
                last.then_inc(turned, 1)
                pe.wait_ge(hx_out, g + 1)
                pe.wait_ge(s_out, g + 1)
                nc.tensor.matmul(psA[:, 0:w], wm2[:], sT[:, 0:w], start=True, stop=False)
                nc.tensor.matmul(psA[:, 0:w], bm2[:], eT[0:1, i0 * P:i0 * P + w], start=False, stop=True).then_inc(agg_ps, 1)
                pe.wait_ge(agg_out, g + 1)
                if g:
                    pe.wait_ge(up_out, g)
                for ps, ww in ((psG, wg), (psU, wu1)):
                    nc.tensor.matmul(ps[:, 0:w], ww[:, 0, :], hT[:, 0:w], start=True, stop=False)
                    nc.tensor.matmul(ps[:, 0:w], ww[:, 1, :], aT[:, 0:w], start=False, stop=True).then_inc(gate_ps, 1)
                pe.wait_ge(up_out, g + 1)
                nc.tensor.matmul(psV[:, 0:w], wu2[:], up[:, 0:w], start=True, stop=True).then_inc(up_ps, 1)
                pe.wait_ge(new_ready, g + 1)
                if g:
                    pe.wait_ge(back_out, g)
                for q in range(n):
                    last = nc.tensor.transpose(psO[:, q, :], new[:, q * P:q * P + P], keep["ident128"][:])
                last.then_inc(back_ps, 1)

        @block.scalar
        def _(act):
            for g, (i0, n) in enumerate(groups):
                w = n * P
                act.wait_ge(turned, g + 1)
                if g:
                    act.wait_ge(new_ready, g)
                    act.wait_ge(gate_ps, 2 * g)
                nc.scalar.copy(hT[:, 0:w], psH[:, 0:w])
                nc.scalar.copy(eT[:, i0 * P:i0 * P + w], psX[:, 0:w]).then_inc(hx_out, 1)
                act.wait_ge(gate_ps, 2 * g + 1)
                nc.scalar.activation(gate[:, 0:w], psG[:, 0:w], ACT.Sigmoid, bias=bg[:]).then_inc(gate_out, 1)
                act.wait_ge(gate_ps, 2 * g + 2)
                if g:
                    act.wait_ge(up_ps, g)
                nc.scalar.activation(up[:, 0:w], psU[:, 0:w], ACT.Relu, bias=bu1[:]).then_inc(up_out, 1)
                act.wait_ge(back_ps, g + 1)
                nc.scalar.copy(o[:, i0:i0 + n, :], psO[:, 0:n, :]).then_inc(back_out, 1)
            norm1.scalar(act)
            norm2.scalar(act)

        @block.vector
        def _(dve):
            link = Serial(dve, chain)
            link(nc.vector.tensor_copy(ext[:, :, 0:17], sums[:, :, 0:17]))
            nc.vector.memset(ext[:, :, 17:18], 1.0).then_inc(ext_ready, 1)
            dve.wait_ge(loads, 160)
            for g, (i0, n) in enumerate(groups):
                w = n * P
                dve.wait_ge(turned, g + 1)
                if g:
                    dve.wait_ge(agg_ps, g)
                nc.vector.tensor_copy(sT[:, 0:w], psS[:, 0:w]).then_inc(s_out, 1)
                dve.wait_ge(agg_ps, g + 1)
                if g:
                    dve.wait_ge(gate_ps, 2 * g)
                nc.vector.tensor_copy(aT[:, 0:w], psA[:, 0:w]).then_inc(agg_out, 1)
                dve.wait_ge(up_ps, g + 1)
                dve.wait_ge(gate_out, g + 1)
                if g:
                    dve.wait_ge(back_ps, g)
                link(nc.vector.scalar_tensor_tensor(out=new[:, 0:w], in0=psV[:, 0:w], scalar=bu2[:], in1=hT[:, 0:w], op0=ALU.add, op1=ALU.subtract))
                link(nc.vector.tensor_tensor(new[:, 0:w], new[:, 0:w], gate[:, 0:w], ALU.mult))
                nc.vector.tensor_tensor(new[:, 0:w], new[:, 0:w], hT[:, 0:w], ALU.add).then_inc(new_ready, 1)
            dve.wait_ge(back_out, len(groups))
            norm1.vector(dve, link, o[:], o[:])
            link(nc.vector.tensor_tensor(o[:], o[:], gamma[:].unsqueeze(1).broadcast_to([P, NT, D]), ALU.mult))
            link(nc.vector.tensor_tensor(o[:], o[:], beta[:].unsqueeze(1).broadcast_to([P, NT, D]), ALU.add))
            nc.vector.tensor_tensor(x[:], x[:], o[:], ALU.add).then_inc(x_ready, 1)
            dve.wait_ge(x_ready, 1)
            norm2.vector(dve, link, h[:], x[:])
            nc.vector.tensor_scalar(h[:], h[:], 0.0, None, ALU.max).then_inc(h_ready, 1)


def turn_counts(nc, t, keep):
    with ExitStack() as ctx:
        sem = lambda n: ctx.enter_context(nc.semaphore(n))
        UB = 5
        row = [ctx.enter_context(nc.sbuf_tensor(f"count_row{u}", [P, N], F16)) for u in range(UB)]
        parts = [(0, 7), (7, 6), (13, 6), (19, 6)]
        ps = [ctx.enter_context(nc.psum_tensor(f"T_ps{b}", [P, 8, 128], F16)) for b in range(4)]
        CT = keep["CT"][:].rearrange("p (s d) -> p s d", d=N)
        loaded = [sem(f"T_loaded{u}") for u in range(UB)]
        turned, out_a, out_v, diag = sem("T_turned"), sem("T_out_a"), sem("T_out_v"), sem("T_diag")
        block = ctx.enter_context(nc.Block())

        @block.sync
        def _(sp):
            with sp.Fori(0, NT // UB) as i:
                for u in range(UB):
                    j = i * UB + u
                    sp.wait_ge(turned, j * 4 + 4)
                    sp.dma_start(row[u][:], t["C"][bass.ds(j * P, P), :]).then_inc(loaded[u], 16)

        @block.tensor
        def _(pe):
            pe.sem_inc(turned, UB * 4)
            with pe.Fori(0, NT // UB) as i:
                for u in range(UB):
                    j = i * UB + u
                    pe.wait_ge(loaded[u], i * 16 + 16)
                    for b, (s0, n) in enumerate(parts):
                        pe.wait_ge(out_a if b % 2 else out_v, j * 2 + b // 2 + 1)
                        for q in range(n):
                            last = nc.tensor.transpose(ps[b][:, q, 0:P], row[u][:, (s0 + q) * P:(s0 + q + 1) * P], keep["ident16"][:])
                        last.then_inc(turned, 1)

        def drain(eng, copy, out, mine):
            eng.sem_inc(out, 2)
            with eng.Fori(0, NT) as j:
                for b in mine:
                    s0, n = parts[b]
                    eng.wait_ge(turned, j * 4 + UB * 4 + b + 1)
                    copy(CT[:, s0:s0 + n, bass.ds(j * P, P)], ps[b][:, 0:n, 0:P]).then_inc(out, 1)

        @block.scalar
        def _(act):
            drain(act, nc.scalar.copy, out_a, (1, 3))

        @block.vector
        def _(dve):
            drain(dve, nc.vector.tensor_copy, out_v, (0, 2))
            dve.wait_ge(out_a, 2 * NT + 2)
            dve.wait_ge(out_v, 2 * NT + 2)
            for j in range(NT):
                last = nc.vector.tensor_tensor(CT[:, j, j * P:(j + 1) * P], CT[:, j, j * P:(j + 1) * P], keep["ident16"][:], ALU.add)
            last.then_inc(diag, 1)


def sage(nc, t, a, keep):
    with ExitStack() as ctx:
        sb = lambda n, s, d: ctx.enter_context(nc.sbuf_tensor(n, s, d))
        pb = lambda n, s, d: ctx.enter_context(nc.psum_tensor(n, s, d))
        sem = lambda n: ctx.enter_context(nc.semaphore(n))
        L = 5
        KW = 447
        cols = [(c, min(KW, N - c)) for c in range(0, N, KW)]
        groups = [(g, min(4, NT - g)) for g in range(0, NT, 4)]
        CT = keep["CT"]
        part = [sb(f"part{m}", [P, NT, D], BF16) for m in range(3)]
        aggT = sb("aggT", [D, N], F32)
        extT = [sb(f"extT{u}", [EXT, KW], F32) for u in range(2)]
        W, b, ew = sb("D_W", [D, L, D], F32), sb("D_b", [P, L * D], F32), sb("D_ew", [EXT, L, D], F32)
        deg, rdeg = sb("D_deg", [P, NT], F32), sb("D_rdeg", [P, NT], F32)
        tmp = [sb(f"D_tmp{u}", [P, 4, D], F32) for u in range(2)]
        psS = pb("D_psS", [D, 7, 512], F32)
        psO = pb("D_psO", [P, 4, D], F32)
        (loads, fresh, ext_ready0, ext_ready1, sums_ps, agg_a, agg_v, out_ps, lin, hi, rest, mid, parts_ready, chain) = (
            sem("D_" + n) for n in ("loads", "fresh", "ext0", "ext1", "sums_ps", "agg_a", "agg_v", "out_ps", "lin",
                                    "hi", "rest", "mid", "parts", "chain"))
        stored = [sem(f"D_stored{u}") for u in range(2)]
        ext_ready = (ext_ready0, ext_ready1)
        G = len(groups)
        block = ctx.enter_context(nc.Block())

        @block.sync
        def _(sp):
            sp.dma_start(W[:], a["Ws"].rearrange("l p n -> p l n")).then_inc(loads, 16)
            sp.dma_start(b[:], a["bs"].rearrange("l n -> (l n)").partition_broadcast(P)).then_inc(loads, 16)
            sp.dma_start(ew[0:1, :, :], a["ebs"].unsqueeze(0)).then_inc(loads, 16)
            sp.dma_start(ew[1:17, :, :], a["ewsT"].rearrange("l f n -> f l n")).then_inc(loads, 16)
            sp.dma_start(ew[17:18, :, :], a["ebs"].unsqueeze(0)).then_inc(loads, 16)
            sp.dma_start(deg[:], t["ext"][0, :].rearrange("(i p) -> p i", p=P), allow_slow_non_contiguous=True).then_inc(loads, 16)
            n = 0
            for l in range(L):
                for q, (c, w) in enumerate(cols):
                    if n >= 2:
                        sp.wait_ge(sums_ps, n - 1)
                    sp.dma_start(extT[n % 2][:, 0:w], t["ext"][:, c:c + w]).then_inc(ext_ready[n % 2], 16)
                    n += 1
            for g, (i0, m) in enumerate(groups):
                sp.wait_ge(lin, (L - 1) * G + g + 1)
                sp.dma_start(rows(t["y"])[:, i0:i0 + m, :], tmp[((L - 1) * G + g) % 2][:, 0:m, :]).then_inc(stored[g % 2], 16)
            for u in range(2):
                sp.wait_ge(stored[u], 16 * ((G + 1 - u) // 2))

        @block.gpsimd
        def _(pool):
            for g, (i0, m) in enumerate(groups):
                if g >= 2:
                    pool.wait_ge(parts_ready, g - 1)
                pool.dma_start(tmp[g % 2][:, 0:m, :], rows(t["h"])[:, i0:i0 + m, :]).then_inc(fresh, 16)
                pool.wait_ge(fresh, 16 * g + 16)

        @block.tensor
        def _(pe):
            pe.wait_ge(loads, 96)
            for l in range(L):
                pe.wait_ge(parts_ready, G * l + G)
                if l:
                    pe.wait_ge(agg_a, 3 * l)
                    pe.wait_ge(agg_v, 4 * l)
                for q, (c, w) in enumerate(cols):
                    nc.tensor.matmul(psS[:, q, 0:w], part[0][:, 0, :], CT[:, c:c + w], start=True, stop=False)
                    for m in (1, 2):
                        nc.tensor.matmul(psS[:, q, 0:w], part[m][:, 0, :], CT[:, c:c + w], start=False, stop=False)
                with pe.Fori(1, NT) as s:
                    for m in range(3):
                        for q, (c, w) in enumerate(cols):
                            nc.tensor.matmul(psS[:, q, 0:w], part[m][:, bass.ds(s, 1), :].squeeze(1), CT[:, bass.ds(s * N + c, w)], start=False, stop=False)
                for q, (c, w) in enumerate(cols):
                    n = l * len(cols) + q
                    pe.wait_ge(ext_ready[n % 2], 16 * (n // 2) + 16)
                    nc.tensor.matmul(psS[:, q, 0:w], ew[:, l, :], extT[n % 2][:, 0:w], start=False, stop=True).then_inc(sums_ps, 1)
                for g, (i0, m) in enumerate(groups):
                    n = l * G + g
                    last_q = ((i0 + m) * P - 1) // KW
                    pe.wait_ge(agg_a, 3 * l + (last_q + 1) // 2) if (last_q + 1) // 2 + 3 * l else None
                    pe.wait_ge(agg_v, 4 * l + last_q // 2 + 1)
                    if n:
                        pe.wait_ge(lin, n)
                    for q in range(m):
                        last = nc.tensor.matmul(psO[:, q, :], aggT[:, (i0 + q) * P:(i0 + q + 1) * P], W[:, l, :], start=True, stop=True)
                    last.then_inc(out_ps, 1)

        @block.scalar
        def _(act):
            for l in range(-1, L):
                if l >= 0:
                    for q, (c, w) in enumerate(cols):
                        if q % 2:
                            act.wait_ge(sums_ps, l * len(cols) + q + 1)
                            if l:
                                act.wait_ge(out_ps, l * G)
                            nc.scalar.copy(aggT[:, c:c + w], psS[:, q, 0:w]).then_inc(agg_a, 1)
                if l == L - 1:
                    break
                for g, (i0, m) in enumerate(groups):
                    n = (l + 1) * G + g
                    if l < 0:
                        act.wait_ge(fresh, 16 * g + 16)
                    else:
                        act.wait_ge(lin, l * G + g + 1)
                    tm = tmp[(g if l < 0 else l * G + g) % 2]
                    if l >= 0:
                        act.wait_ge(sums_ps, (l + 1) * len(cols))
                    nc.scalar.activation(part[0][:, i0:i0 + m, :], tm[:, 0:m, :], ACT.Relu).then_inc(hi, 1)
                    act.wait_ge(rest, n + 1)
                    nc.scalar.copy(part[1][:, i0:i0 + m, :], tm[:, 0:m, :]).then_inc(mid, 1)

        @block.vector
        def _(dve):
            link = Serial(dve, chain)
            dve.wait_ge(loads, 96)
            link(nc.vector.tensor_scalar(deg[:], deg[:], 1.0, None, ALU.add))
            link(nc.vector.reciprocal(rdeg[:], deg[:]))
            for l in range(-1, L):
                if l >= 0:
                    for q, (c, w) in enumerate(cols):
                        if q % 2 == 0:
                            dve.wait_ge(sums_ps, l * len(cols) + q + 1)
                            if l:
                                dve.wait_ge(out_ps, l * G)
                            nc.vector.tensor_copy(aggT[:, c:c + w], psS[:, q, 0:w]).then_inc(agg_v, 1)
                for g, (i0, m) in enumerate(groups):
                    n = (l + 1) * G + g
                    tm = tmp[(g if l < 0 else l * G + g) % 2]
                    if l >= 0:
                        dve.wait_ge(out_ps, l * G + g + 1)
                        dve.wait_ge(parts_ready, min(n - 1, L * G) if l > 0 or g >= 2 else G)
                        if l == L - 1 and g >= 2:
                            dve.wait_ge(stored[g % 2], 16 * (g // 2))
                        for q in range(m):
                            last = nc.vector.scalar_tensor_tensor(out=tm[:, q, :], in0=psO[:, q, :], scalar=rdeg[:, i0 + q:i0 + q + 1], in1=b[:, l * D:(l + 1) * D], op0=ALU.mult, op1=ALU.add)
                        last.then_inc(lin, 1)
                        dve.wait_ge(lin, l * G + g + 1)
                    else:
                        dve.wait_ge(fresh, 16 * g + 16)
                    if l == L - 1:
                        continue
                    dve.wait_ge(hi, n + 1)
                    nc.vector.scalar_tensor_tensor(out=tm[:, 0:m, :], in0=tm[:, 0:m, :], scalar=0.0, in1=part[0][:, i0:i0 + m, :], op0=ALU.max, op1=ALU.subtract).then_inc(rest, 1)
                    dve.wait_ge(mid, n + 1)
                    nc.vector.tensor_tensor(part[2][:, i0:i0 + m, :], tm[:, 0:m, :], part[1][:, i0:i0 + m, :], ALU.subtract).then_inc(parts_ready, 1)


def residual(nc, t, a, keep, name, bias=None):
    with ExitStack() as ctx:
        sb = lambda n, s, d: ctx.enter_context(nc.sbuf_tensor(f"{name}_{n}", s, d))
        sem = lambda n: ctx.enter_context(nc.semaphore(f"{name}_{n}"))
        x, y = sb("x", [P, NT, D], F32), sb("y", [P, NT, D], F32)
        bb = sb("bias", [P, D], F32)
        loads, x_ready, h_ready, chain, stored = sem("loads"), sem("x_ready"), sem("h_ready"), sem("chain"), sem("stored")
        norm = Norm(nc, ctx, name)
        n_loads = 2 + (bias is not None)
        block = ctx.enter_context(nc.Block())

        @block.sync
        def _(sp):
            sp.dma_start(x[:], rows(t["x"])).then_inc(loads, 16)
            sp.dma_start(y[:], rows(t["y"])).then_inc(loads, 16)
            if bias is not None:
                sp.dma_start(bb[:], a[bias].partition_broadcast(P)).then_inc(loads, 16)
            sp.wait_ge(x_ready, 1)
            sp.dma_start(rows(t["x"]), x[:]).then_inc(stored, 16)
            sp.wait_ge(h_ready, 1)
            sp.dma_start(rows(t["h"]), y[:]).then_inc(stored, 16)
            sp.wait_ge(stored, 32)

        @block.scalar
        def _(act):
            norm.scalar(act)

        @block.vector
        def _(dve):
            link = Serial(dve, chain)
            dve.wait_ge(loads, 16 * n_loads)
            if bias is not None:
                link(nc.vector.tensor_tensor(y[:], y[:], bb[:].unsqueeze(1).broadcast_to([P, NT, D]), ALU.add))
            nc.vector.tensor_tensor(x[:], x[:], y[:], ALU.add).then_inc(x_ready, 1)
            dve.wait_ge(x_ready, 1)
            norm.vector(dve, link, y[:], x[:])
            nc.vector.tensor_scalar(y[:], y[:], 0.0, None, ALU.max).then_inc(h_ready, 1)


def project_in(nc, t, a, keep):
    with ExitStack() as ctx:
        sb = lambda n, s, d: ctx.enter_context(nc.sbuf_tensor(n, s, d))
        pb = lambda n, s, d: ctx.enter_context(nc.psum_tensor(n, s, d))
        sem = lambda n: ctx.enter_context(nc.semaphore("E1_" + n))
        h = keep["ha"]
        hT = sb("E1_hT", [D, 2, P], F32)
        WT, av, va = sb("E1_WT", [D, 2, D], F32), sb("E1_av", [D, 2, 2], F32), sb("E1_va", [D, 2], F32)
        psT, psV, psC = pb("E1_psT", [D, 2, 512], F32), pb("E1_psV", [D, 512], F32), pb("E1_psC", [P, NT, 2], F32)
        loads, turned, out, va_ps, va_ready, col_ps, ready = (sem(n) for n in ("loads", "turned", "out", "va_ps", "va_ready", "col_ps", "ready"))
        block = ctx.enter_context(nc.Block())

        @block.sync
        def _(sp):
            sp.dma_start(h[:, :, 0:D], rows(t["h"])).then_inc(loads, 16)
            sp.dma_start(WT[:], a["W1T"].rearrange("(k p) n -> p k n", p=D)).then_inc(loads, 16)
            sp.dma_start(av[:, :, 0:1], a["a1_src"].rearrange("(k p o) -> p k o", p=D, o=1), allow_slow_non_contiguous=True).then_inc(loads, 16)
            sp.dma_start(av[:, :, 1:2], a["a1_dst"].rearrange("(k p o) -> p k o", p=D, o=1), allow_slow_non_contiguous=True).then_inc(loads, 16)

        @block.tensor
        def _(pe):
            pe.wait_ge(loads, 64)
            for k in range(2):
                last = nc.tensor.matmul(psV[:, 0:2], WT[:, k, :], av[:, k, :], start=k == 0, stop=k == 1)
            last.then_inc(va_ps, 1)
            pe.wait_ge(va_ready, 1)
            for j in range(NT):
                if j >= 2:
                    pe.wait_ge(out, j - 1)
                nc.tensor.transpose(psT[:, j % 2, 0:P], h[:, j, 0:D], keep["ident32"][:]).then_inc(turned, 1)
                pe.wait_ge(out, j + 1)
                nc.tensor.matmul(psC[:, j, :], hT[:, j % 2, :], va[:], start=True, stop=True).then_inc(col_ps, 1)

        @block.scalar
        def _(act):
            act.wait_ge(va_ps, 1)
            nc.scalar.copy(va[:], psV[:, 0:2]).then_inc(va_ready, 1)
            for j in range(NT):
                act.wait_ge(turned, j + 1)
                if j >= 2:
                    act.wait_ge(col_ps, j - 1)
                nc.scalar.copy(hT[:, j % 2, :], psT[:, j % 2, 0:P]).then_inc(out, 1)

        @block.vector
        def _(dve):
            nc.vector.memset(h[:, :, D:D + 1], 1.0).then_inc(ready, 1)
            dve.wait_ge(col_ps, NT)
            nc.vector.tensor_copy(keep["a_col"][:], psC[:].rearrange("p j k -> p k j")).then_inc(ready, 1)


def attend(nc, t, a, keep, name):
    with ExitStack() as ctx:
        sb = lambda n, s, d: ctx.enter_context(nc.sbuf_tensor(f"{name}_{n}", s, d))
        pb = lambda n, s, d: ctx.enter_context(nc.psum_tensor(f"{name}_{n}", s, d))
        sem = lambda n: ctx.enter_context(nc.semaphore(f"{name}_{n}"))
        CB = 5
        CW = CB * P
        NCH = NT // CB
        ha, CT = keep["ha"], keep["CT"]
        a_s, a_d = keep["a_col"][:, 0, :], keep["a_col"][:, 1, :]
        acc = sb("acc", [P, N], F32)
        w = [acc[:, u * CW:(u + 1) * CW] for u in range(5)]
        col = sb("col", [P, 8, NT], F32)
        big, pos, as8, as2, mx, m, low = (col[:, n, :] for n in range(7))
        b12 = sb("b12", [P, 2, NT], F32)
        one = sb("one", [P, 8], F32)
        diag = sb("diag", [P, 2 * CB, P], F32)
        ones, zeros = sb("ones", [P, P], F32), sb("zeros", [P, P], F32)
        row = sb("row", [P, 2, 2, CW], F32)
        rz = sb("rz", [P, CB], F32)
        o = sb("o", [P, CB, D], F32)
        DA = D + 1
        psO = [[pb(f"psO{v}{r}", [P, 512], F32) for r in range(2)] for v in range(2)]
        psB = pb("psB", [P, 4, 512], F32)
        (chain, amax, amax_all, masked, turned, mx_out, consts, diag_ready, row_ps, row_ready, x_ready, e_ready,
         w_ready, w_used, sum_ps, o_ready, o_stored) = (sem(n) for n in (
            "chain", "amax", "amax_all", "masked", "turned", "mx_out", "consts", "diag_ready", "row_ps", "row_ready",
            "x_ready", "e_ready", "w_ready", "w_used", "sum_ps", "o_ready", "o_stored"))
        block = ctx.enter_context(nc.Block())

        def place(j):
            return j // 3, (j % 3) * DA

        @block.gpsimd
        def _(pool):
            pool.wait_ge(amax, 1)
            nc.gpsimd.partition_all_reduce(one[:, 1:2], one[:, 0:1], P, RMAX).then_inc(amax_all, 1)

        @block.sync
        def _(sp):
            for c in range(NCH):
                sp.wait_ge(o_ready, c + 1)
                sp.dma_start(rows(t["y"])[:, c * CB:(c + 1) * CB, :], o[:]).then_inc(o_stored, 16)
                sp.wait_ge(o_stored, 16 * c + 16)

        @block.vector
        def _(dve):
            link = Serial(dve, chain)
            link(nc.vector.memset(ones[:], 1.0))
            link(nc.vector.memset(zeros[:], 0.0))
            link(nc.vector.memset(acc[:], 0.0))
            link(nc.vector.tensor_reduce(one[:, 4:5], a_s, AX.X, ALU.max, apply_absolute_value=True))
            nc.vector.tensor_scalar(one[:, 0:1], one[:, 4:5], 1e-30, None, ALU.max).then_inc(amax, 1)
            dve.wait_ge(amax_all, 1)
            link(nc.vector.reciprocal(one[:, 2:3], one[:, 1:2]))
            link(nc.vector.tensor_scalar(big, a_s, one[:, 2:3], 0.25, ALU.mult, ALU.mult))
            link(nc.vector.tensor_scalar(pos, big, 0.5, None, ALU.add))
            link(nc.vector.tensor_scalar(as8, a_s, 0.8, None, ALU.mult))
            link(nc.vector.tensor_scalar(as2, a_s, 0.2, None, ALU.mult))
            base = link.n
            with dve.Fori(0, NT) as s:
                step = Serial(dve, chain, base + s)
                step(nc.vector.scalar_tensor_tensor(out=acc[:], in0=CT[:, bass.ds(s * N, N)], scalar=pos[:, bass.ds(s, 1)],
                                                    in1=acc[:], op0=ALU.min, op1=ALU.max))
            link.n += NT
            dve.sem_inc(masked, 1)
            for g in range(0, NT, 4):
                n = min(4, NT - g)
                b = (g // 4) % 4
                dve.wait_ge(turned, g // 4 + 1)
                nc.vector.tensor_reduce(mx[:, g:g + n], psB[:, b, 0:n * P].rearrange("p (j s) -> p j s", s=P), AX.X, ALU.max).then_inc(mx_out, 1)
            dve.wait_ge(mx_out, (NT + 3) // 4)
            link(nc.vector.tensor_scalar(mx, mx, -0.5, 4.0, ALU.add, ALU.mult))
            link(nc.vector.scalar_tensor_tensor(out=mx, in0=mx, scalar=one[:, 1:2], in1=a_d, op0=ALU.mult, op1=ALU.add))
            link(nc.vector.scalar_tensor_tensor(out=m, in0=mx, scalar=0.2, in1=mx, op0=ALU.mult, op1=ALU.max))
            link(nc.vector.tensor_tensor(b12[:, 0, :], a_d, m, ALU.subtract))
            link(nc.vector.scalar_tensor_tensor(out=b12[:, 1, :], in0=a_d, scalar=0.2, in1=m, op0=ALU.mult, op1=ALU.subtract))

            def diagonals(c):
                if c:
                    dve.wait_ge(row_ps, c)
                for r in range(2):
                    for j in range(CB):
                        last = nc.vector.tensor_scalar(diag[:, r * CB + j, :], keep["ident32"][:], b12[:, r, c * CB + j:c * CB + j + 1], None, ALU.mult)
                last.then_inc(diag_ready, 1)

            diagonals(0)
            dve.sem_inc(w_ready, 1)
            for c in range(NCH):
                if c + 1 < NCH:
                    diagonals(c + 1)
                dve.wait_ge(row_ready, c + 1)
                with dve.Fori(0, NT // 5) as i:
                    for u in range(5):
                        s = i * 5 + u
                        dve.wait_ge(w_used, s + (c * NT + 1))
                        nc.vector.scalar_tensor_tensor(out=w[u], in0=row[:, c % 2, 0, :], scalar=as8[:, bass.ds(s, 1)],
                                                       in1=row[:, c % 2, 1, :], op0=ALU.add, op1=ALU.max).then_inc(x_ready, 1)
                    for u in range(5):
                        s = i * 5 + u
                        dve.wait_ge(e_ready, s + (c * NT + 1))
                        nc.vector.scalar_tensor_tensor(out=w[u], in0=w[u], scalar=2.0, in1=CT[:, bass.ds(s * N + c * CW, CW)],
                                                       op0=ALU.min, op1=ALU.mult).then_inc(w_ready, 1)
                dve.wait_ge(sum_ps, c + 1)
                if c:
                    dve.wait_ge(o_stored, 16 * c)
                for j in range(CB):
                    r, at = place(j)
                    last = nc.vector.reciprocal(rz[:, j:j + 1], psO[c % 2][r][:, at + D:at + DA])
                link(last)
                for j in range(CB):
                    r, at = place(j)
                    last = nc.vector.tensor_scalar(o[:, j, :], psO[c % 2][r][:, at:at + D], rz[:, j:j + 1], None, ALU.mult)
                last.then_inc(o_ready, 1)
                dve.wait_ge(o_ready, c + 1)

        @block.scalar
        def _(act):
            def make_rows(c):
                act.wait_ge(row_ps, c + 1)
                if c >= 2:
                    act.wait_ge(x_ready, NT * (c - 1))
                for r in range(2):
                    nc.scalar.copy(row[:, c % 2, r, 0:4 * P], psB[:, 2 * r, 0:4 * P])
                    last = nc.scalar.copy(row[:, c % 2, r, 4 * P:CW], psB[:, 2 * r + 1, 0:P])
                last.then_inc(row_ready, 1)

            make_rows(0)
            for c in range(NCH):
                if c + 1 < NCH:
                    make_rows(c + 1)
                with act.Fori(0, NT // 5) as i:
                    for u in range(5):
                        s = i * 5 + u
                        act.wait_ge(x_ready, s + (c * NT + 1))
                        nc.scalar.activation(w[u], w[u], ACT.Exp, bias=as2[:, bass.ds(s, 1)]).then_inc(e_ready, 1)

        @block.tensor
        def _(pe):
            pe.sem_inc(w_used, 5)
            pe.wait_ge(masked, 1)
            for g in range(0, NT, 4):
                n = min(4, NT - g)
                b = (g // 4) % 4
                if g >= 16:
                    pe.wait_ge(mx_out, g // 4 - 3)
                for q in range(n):
                    last = nc.tensor.transpose(psB[:, b, q * P:(q + 1) * P], acc[:, (g + q) * P:(g + q + 1) * P], keep["ident32"][:])
                last.then_inc(turned, 1)
            pe.wait_ge(mx_out, (NT + 3) // 4)

            def spread(c):
                pe.wait_ge(diag_ready, c + 1)
                if c:
                    pe.wait_ge(row_ready, c)
                for r in range(2):
                    for j in range(CB):
                        last = nc.tensor.matmul(psB[:, 2 * r + j // 4, (j % 4) * P:(j % 4 + 1) * P], ones[:], diag[:, r * CB + j, :], start=True, stop=True)
                last.then_inc(row_ps, 1)

            def clear(c, start):
                flat = ha[:].rearrange("p j f -> p (j f)")
                for r, n in ((0, 3), (1, 2)):
                    last = nc.tensor.matmul(psO[c % 2][r][:, 0:n * DA], zeros[:], flat[:, 0:n * DA], start=start, stop=not start)
                return last

            spread(0)
            for c in range(NCH):
                if c + 1 < NCH:
                    spread(c + 1)
                if c >= 2:
                    pe.wait_ge(o_ready, c - 1)
                clear(c, True)
                with pe.Fori(0, NT // 5) as i:
                    for u in range(5):
                        s = i * 5 + u
                        pe.wait_ge(w_ready, s + (c * NT + 2))
                        for j in range(CB):
                            r, at = place(j)
                            last = nc.tensor.matmul(psO[c % 2][r][:, at:at + DA], w[u][:, j * P:(j + 1) * P], ha[:, bass.ds(s, 1), :].squeeze(1),
                                                    start=False, stop=False)
                        last.then_inc(w_used, 1)
                clear(c, False).then_inc(sum_ps, 1)


def between(nc, t, a, keep):
    with ExitStack() as ctx:
        sb = lambda n, s, d: ctx.enter_context(nc.sbuf_tensor("M_" + n, s, d))
        pb = lambda n, s, d: ctx.enter_context(nc.psum_tensor("M_" + n, s, d))
        sem = lambda n: ctx.enter_context(nc.semaphore("M_" + n))
        groups = [(g, min(4, NT - g)) for g in range(0, NT, 4)]
        GW = 4 * P
        W1, W2, W2T = sb("W1", [D, 2 * D], F32), sb("W2", [D, 2, D + 2], F32), sb("W2T", [D, 2 * D], F32)
        av, b1 = sb("av", [D, 2], F32), sb("b1", [D, 2], F32)
        y = [sb(f"y{u}", [P, 4, D], F32) for u in range(2)]
        yT, r = sb("yT", [D, GW], F32), sb("r", [D, 2, GW], F32)
        psV, psT, psR = pb("psV", [D, 2, 2], F32), pb("psT", [D, 512], F32), pb("psR", [D, 2, 512], F32)
        psZ = pb("psZ", [P, 4, 512], F32)
        loads, va_ps, va_ready, turned, t_out, r_ps, r_out, z_ps, z_out = (
            sem(n) for n in ("loads", "va_ps", "va_ready", "turned", "t_out", "r_ps", "r_out", "z_ps", "z_out"))
        y_ready = [sem(f"y_ready{u}") for u in range(2)]
        block = ctx.enter_context(nc.Block())

        @block.sync
        def _(sp):
            sp.dma_start(W1[:], a["W1"]).then_inc(loads, 16)
            sp.dma_start(W2[:, :, 0:D], a["W2"].rearrange("(k p) n -> p k n", p=D)).then_inc(loads, 16)
            sp.dma_start(W2T[:], a["W2T"]).then_inc(loads, 16)
            sp.dma_start(av[:, 0:1], a["a2_src"].unsqueeze(1)).then_inc(loads, 16)
            sp.dma_start(av[:, 1:2], a["a2_dst"].unsqueeze(1)).then_inc(loads, 16)
            for k in range(2):
                sp.dma_start(b1[:, k:k + 1], a["b1"][k * D:(k + 1) * D].unsqueeze(1)).then_inc(loads, 16)
            for g, (i0, n) in enumerate(groups):
                if g >= 2:
                    sp.wait_ge(turned, g - 1)
                sp.dma_start(y[g % 2][:, 0:n, :], rows(t["y"])[:, i0:i0 + n, :]).then_inc(y_ready[g % 2], 16)

        @block.tensor
        def _(pe):
            pe.wait_ge(loads, 112)
            for k in range(2):
                last = nc.tensor.matmul(psV[:, k, :], W2T[:, k * D:(k + 1) * D], av[:], start=True, stop=True)
            last.then_inc(va_ps, 1)
            for g, (i0, n) in enumerate(groups):
                w = n * P
                pe.wait_ge(y_ready[g % 2], 16 * (g // 2) + 16)
                if g:
                    pe.wait_ge(t_out, g)
                for q in range(n):
                    last = nc.tensor.transpose(psT[:, q * P:(q + 1) * P], y[g % 2][:, q, :], keep["ident32"][:])
                last.then_inc(turned, 1)
                pe.wait_ge(t_out, g + 1)
                if g:
                    pe.wait_ge(r_out, g)
                for k in range(2):
                    last = nc.tensor.matmul(psR[:, k, 0:w], W1[:, k * D:(k + 1) * D], yT[:, 0:w], start=True, stop=True)
                last.then_inc(r_ps, 1)
                pe.wait_ge(r_out, g + 1)
                pe.wait_ge(va_ready, 1)
                if g:
                    pe.wait_ge(z_out, g)
                for q in range(n):
                    for k in range(2):
                        last = nc.tensor.matmul(psZ[:, q, 0:D + 2], r[:, k, q * P:(q + 1) * P], W2[:, k, :], start=k == 0, stop=k == 1)
                last.then_inc(z_ps, 1)

        @block.scalar
        def _(act):
            for g, (i0, n) in enumerate(groups):
                w = n * P
                act.wait_ge(r_ps, g + 1)
                if g:
                    act.wait_ge(z_ps, g)
                for k in range(2):
                    last = nc.scalar.activation(r[:, k, 0:w], psR[:, k, 0:w], ACT.Relu, bias=b1[:, k:k + 1])
                last.then_inc(r_out, 1)

        @block.vector
        def _(dve):
            dve.wait_ge(va_ps, 1)
            nc.vector.tensor_copy(W2[:, :, D:D + 2], psV[:]).then_inc(va_ready, 1)
            for g, (i0, n) in enumerate(groups):
                w = n * P
                dve.wait_ge(turned, g + 1)
                if g:
                    dve.wait_ge(r_ps, g)
                nc.vector.tensor_copy(yT[:, 0:w], psT[:, 0:w]).then_inc(t_out, 1)
                dve.wait_ge(z_ps, g + 1)
                nc.vector.tensor_copy(keep["ha"][:, i0:i0 + n, 0:D], psZ[:, 0:n, 0:D])
                nc.vector.tensor_copy(keep["a_col"][:, :, i0:i0 + n], psZ[:, 0:n, D:D + 2].rearrange("p j k -> p k j")).then_inc(z_out, 1)


def project_heads(nc, t, a, keep):
    with ExitStack() as ctx:
        sb = lambda n, s, d: ctx.enter_context(nc.sbuf_tensor("F1_" + n, s, d))
        pb = lambda n, s, d: ctx.enter_context(nc.psum_tensor("F1_" + n, s, d))
        sem = lambda n: ctx.enter_context(nc.semaphore("F1_" + n))
        h, hT = sb("h", [P, NT, D], F32), sb("hT", [D, 2, P], F32)
        WT, W, att = sb("WT", [D, D], F32), sb("W", [D, D + 2 * HEADS], F32), sb("att", [D, 2 * HEADS], F32)
        tab = sb("tab", [P, NT, HEADS, RW], F32)
        psT, psW, psZ = pb("psT", [D, 2, 512], F32), pb("psW", [D, 2 * HEADS], F32), pb("psZ", [P, 2, 512], F32)
        loads, cleared, w_ps, w_ready, turned, out, z_ps, z_out, stored = (
            sem(n) for n in ("loads", "cleared", "w_ps", "w_ready", "turned", "out", "z_ps", "z_out", "stored"))
        block = ctx.enter_context(nc.Block())

        @block.sync
        def _(sp):
            sp.dma_start(h[:], rows(t["h"])).then_inc(loads, 16)
            sp.dma_start(WT[:], a["W3T"]).then_inc(loads, 16)
            sp.dma_start(W[:, 0:D], a["W3"]).then_inc(loads, 16)
            sp.wait_ge(cleared, 1)
            for k in range(2):
                for g in range(HEADS):
                    sp.dma_start(att[g * HC:(g + 1) * HC, k * HEADS + g:k * HEADS + g + 1], a["att"][g, k * HC:(k + 1) * HC].unsqueeze(1)).then_inc(loads, 16)
            sp.wait_ge(z_out, NT)
            for g in range(HEADS):
                sp.dma_start(rows(t["tab"][g * N:(g + 1) * N, :]), tab[:, :, g, :]).then_inc(stored, 16)
            sp.wait_ge(stored, 16 * HEADS)

        @block.tensor
        def _(pe):
            pe.wait_ge(loads, 16 * (3 + 2 * HEADS))
            nc.tensor.matmul(psW[:], WT[:], att[:], start=True, stop=True).then_inc(w_ps, 1)
            pe.wait_ge(w_ready, 1)
            for j in range(NT):
                if j >= 2:
                    pe.wait_ge(out, j - 1)
                    pe.wait_ge(z_out, j - 1)
                nc.tensor.transpose(psT[:, j % 2, 0:P], h[:, j, :], keep["ident32"][:]).then_inc(turned, 1)
                pe.wait_ge(out, j + 1)
                nc.tensor.matmul(psZ[:, j % 2, 0:D + 2 * HEADS], hT[:, j % 2, :], W[:], start=True, stop=True).then_inc(z_ps, 1)

        @block.scalar
        def _(act):
            for j in range(NT):
                act.wait_ge(turned, j + 1)
                if j >= 2:
                    act.wait_ge(z_ps, j - 1)
                nc.scalar.copy(hT[:, j % 2, :], psT[:, j % 2, 0:P]).then_inc(out, 1)

        @block.vector
        def _(dve):
            nc.vector.memset(att[:], 0.0).then_inc(cleared, 1)
            dve.wait_ge(w_ps, 1)
            nc.vector.tensor_copy(W[:, D:D + 2 * HEADS], psW[:]).then_inc(w_ready, 1)
            for j in range(NT):
                dve.wait_ge(z_ps, j + 1)
                z = psZ[:, j % 2, :]
                nc.vector.tensor_copy(tab[:, j, :, 0:HC], z[:, 0:D].rearrange("p (g c) -> p g c", c=HC))
                nc.vector.tensor_copy(tab[:, j, :, HC:RW], z[:, D + HEADS:D + 2 * HEADS].unsqueeze(2))
                nc.vector.tensor_copy(keep["ai"][:, :, j:j + 1], z[:, D:D + HEADS].unsqueeze(2))
                nc.vector.tensor_copy(keep["aj"][:, :, j:j + 1], z[:, D + HEADS:D + 2 * HEADS].unsqueeze(2)).then_inc(z_out, 1)


def rank(nc, t, a, keep):
    with ExitStack() as ctx:
        sb = lambda n, s, d: ctx.enter_context(nc.sbuf_tensor("F2_" + n, s, d))
        pb = lambda n, s, d: ctx.enter_context(nc.psum_tensor("F2_" + n, s, d))
        sem = lambda n: ctx.enter_context(nc.semaphore("F2_" + n))
        diag, row = sb("diag", [P, N], F32), sb("row", [P, N], F32)
        junk_a, junk_v = sb("junk_a", [P, N], F16), sb("junk_v", [P, N], F16)
        ones = sb("ones", [P, P], F32)
        rho, hi = sb("rho", [P, HEADS * NT], F32), sb("hi", [P, HEADS * NT], F16)
        psR = pb("psR", [P, N], F32)
        CT = keep["CT"]
        order = [HEADS - 1] + list(range(HEADS - 1))
        chain, diag_ready, row_ps, row_out, signs = (sem(n) for n in ("chain", "diag_ready", "row_ps", "row_out", "signs"))
        block = ctx.enter_context(nc.Block())

        @block.tensor
        def _(pe):
            for n, g in enumerate(order):
                pe.wait_ge(diag_ready, n + 1)
                if n == 1:
                    pe.wait_ge(row_out, 1)
                elif n:
                    pe.wait_ge(signs, NT * (n - 1))
                for c in range(0, N, 512):
                    w = min(512, N - c)
                    last = nc.tensor.matmul(psR[:, c:c + w], ones[:], diag[:, c:c + w], start=True, stop=True)
                last.then_inc(row_ps, 1)

        @block.scalar
        def _(act):
            for n, g in enumerate(order[1:]):
                act.wait_ge(row_ps, n + 2)
                for j in range(NT):
                    at = g * NT + j
                    if n or j:
                        act.wait_ge(signs, n * NT + j)
                    nc.scalar.activation(junk_a[:], psR[:], ACT.Sign, bias=keep["aj"][:, g, j:j + 1], scale=-1.0,
                                         accum_out=rho[:, at:at + 1]).then_inc(signs, 1)

        @block.vector
        def _(dve):
            link = Serial(dve, chain)
            link(nc.vector.memset(ones[:], 1.0))

            def diagonals(n, g):
                if n:
                    dve.wait_ge(row_ps, n)
                for j in range(NT):
                    last = nc.vector.tensor_scalar(diag[:, j * P:(j + 1) * P], keep["ident32"][:], keep["aj"][:, g, j:j + 1], None, ALU.mult)
                last.then_inc(diag_ready, 1)

            def count_less(j):
                link(nc.vector.tensor_scalar(junk_v[:], row[:], keep["aj"][:, order[0], j:j + 1], 0.0, ALU.is_lt, ALU.add,
                                             accum_out=rho[:, order[0] * NT + j:order[0] * NT + j + 1]))

            def make_ready(s):
                c = CT[:, s * N:(s + 1) * N]
                link(nc.vector.tensor_scalar(junk_v[:], c, 0.0, ABSENT, ALU.is_equal, ALU.mult))
                link(nc.vector.tensor_scalar(c, c, float(TOP), None, ALU.min))
                link(nc.vector.tensor_tensor(c, c, junk_v[:], ALU.add))

            diagonals(0, order[0])
            dve.wait_ge(row_ps, 1)
            nc.vector.tensor_copy(row[:], psR[:]).then_inc(row_out, 1)
            dve.wait_ge(row_out, 1)
            diagonals(1, order[1])
            for j in range(NT):
                count_less(j)
            diagonals(2, order[2])
            for s in range(NT):
                if s == 12:
                    diagonals(3, order[3])
                make_ready(s)
            dve.wait_ge(signs, NT * (HEADS - 1))
            link(nc.vector.tensor_copy(hi[:], rho[:]))
            link(nc.vector.tensor_copy(keep["rank"][:, 0, :], hi[:]))
            link(nc.vector.tensor_tensor(keep["rank"][:, 1, :], rho[:], keep["rank"][:, 0, :], ALU.subtract))


def top_attention(nc, t, a, keep):
    with ExitStack() as ctx:
        sb = lambda n, s, d: ctx.enter_context(nc.sbuf_tensor("F3_" + n, s, d))
        pb = lambda n, s, d: ctx.enter_context(nc.psum_tensor("F3_" + n, s, d))
        sem = lambda n: ctx.enter_context(nc.semaphore("F3_" + n))
        CT = keep["CT"]
        KW = 447
        cols = [(c, min(KW, N - c)) for c in range(0, N, KW)]
        Q = len(cols)
        GT = 5
        NG = NT // GT
        W8 = GT * TOP
        U32 = mybir.dt.uint32
        drow = sb("diag", [P, 2, N], F16)
        eights = sb("eights", [P, P], F16)
        key = [sb(f"key{u}", [P, N], F32) for u in range(2)]
        top, found, index = sb("top", [P, NT * TOP], F32), sb("found", [P, NT * TOP], U32), sb("index", [P, NT * TOP], I32)
        got = [sb(f"got{u}", [P, W8, RW], F32) for u in range(2)]
        small = [sb(f"small{n}", [P, W8], F32) for n in range(6)]
        ints = [sb(f"ints{n}", [P, W8], I32) for n in range(2)]
        den = sb("den", [P, 2, GT], F32)
        o = [sb(f"o{u}", [P, GT, HC], F32) for u in range(2)]
        head_base = sb("head_base", [P, HEADS], F32)
        psK = pb("psK", [P, Q, 512], F32)
        (chain, based, d_ready, key_ps, key_out, picked, idx_ready, mixed, z_ready, e_ready, o_ready, o_stored, tick, sp_tick, go) = (
            sem(n) for n in ("chain", "based", "d_ready", "key_ps", "key_out", "picked", "idx_ready", "mixed", "z_ready",
                             "e_ready", "o_ready", "o_stored", "tick", "sp_tick", "go"))
        gathered = [sem(f"gathered{u}") for u in range(2)]
        CHAIN = NT + NG * 18
        block = ctx.enter_context(nc.Block())

        @block.sync
        def _(sp):
            sp.sem_inc(o_stored, 16)
            with sp.Fori(0, HEADS) as g:
                y = rows(t["y"]).rearrange("p i (g c) -> p i g c", c=HC)[:, :, bass.ds(g, 1), :].squeeze(2)
                for grp in range(NG):
                    sp.wait_ge(o_ready, g * NG + grp + 1)
                    sp.sem_inc(sp_tick, 1)
                    sp.wait_ge(o_stored, g * (NG * 16) + grp * 16 + 16)
                    sp.sem_inc(sp_tick, 1)
                    sp.dma_start(y[:, grp * GT:(grp + 1) * GT, :], o[grp % 2][:]).then_inc(o_stored, 16)
            sp.wait_ge(o_stored, 16 * HEADS * NG + 16)

        @block.gpsimd
        def _(pool):
            nc.gpsimd.iota(head_base[:], pattern=[[N, HEADS]], base=0, channel_multiplier=0, allow_small_or_imprecise_dtypes=True).then_inc(based, 1)
            with pool.Fori(0, HEADS) as g:
                for u in range(NT):
                    grp = u // GT
                    if u % GT == 0:
                        pool.wait_ge(mixed, g * NG + grp + (1 if grp else 2))
                    pool.wait_ge(idx_ready, g * NT + u + 1)
                    pool.sem_inc(go, 1)
                    for i in range(TOP):
                        nc.gpsimd.indirect_dma_start(
                            out=got[grp % 2][:, (u % GT) * TOP + i, :], out_offset=None, in_=t["tab"],
                            in_offset=bass.IndirectOffsetOnAxis(ap=index[:, u * TOP + i:u * TOP + i + 1], axis=0),
                        ).then_inc(gathered[grp % 2], 16)

        @block.tensor
        def _(pe):
            pe.sem_inc(key_ps, Q)
            with pe.Fori(0, HEADS) as g:
                pe.wait_ge(d_ready, g + 1)
                for u in range(NT):
                    for q, (c, w) in enumerate(cols):
                        pe.wait_ge(key_out, g * (NT * Q) + u * Q + q + 1)
                        nc.tensor.matmul(psK[:, q, 0:w], keep["ident16"][:], CT[:, u * N + c:u * N + c + w], start=True, stop=False)
                        nc.tensor.matmul(psK[:, q, 0:w], eights[:], drow[:, 0, c:c + w], start=False, stop=False)
                        nc.tensor.matmul(psK[:, q, 0:w], eights[:], drow[:, 1, c:c + w], start=False, stop=True).then_inc(key_ps, 1)

        @block.scalar
        def _(act):
            act.sem_inc(key_out, Q)
            act.sem_inc(e_ready, 1)
            with act.Fori(0, HEADS) as g:
                for u in range(NT):
                    act.wait_ge(picked, g * NT + u + (1 if u else 2))
                    for q, (c, w) in enumerate(cols):
                        act.wait_ge(key_ps, g * (NT * Q) + u * Q + q + 1 + Q)
                        nc.scalar.copy(key[u % 2][:, c:c + w], psK[:, q, 0:w]).then_inc(key_out, 1)
                    for grp in range(NG):
                        if u == min(GT * grp + 7, NT - 1):
                            act.wait_ge(z_ready, g * NG + grp + 1)
                            nc.scalar.activation(small[3][:], small[3][:], ACT.Exp).then_inc(e_ready, 1)

        @block.vector
        def _(dve):
            dve.sem_inc(picked, 2)
            dve.sem_inc(mixed, 2)
            nc.vector.memset(eights[:], 8.0).then_inc(tick, 1)
            dve.wait_ge(tick, 1)
            dve.wait_ge(based, 1)
            incl, cnt, take, e, r, z = small
            ti, tj = ints
            v = nc.vector
            with dve.Fori(0, HEADS) as g:
                link = Serial(dve, chain, g * CHAIN)
                dve.wait_ge(key_ps, g * (NT * Q) + Q)
                for j in range(NT):
                    for k in range(2):
                        last = v.tensor_scalar(drow[:, k, j * P:(j + 1) * P], keep["ident16"][:],
                                               keep["rank"][:, k, bass.ds(g * NT + j, 1)], None, ALU.mult)
                last.then_inc(d_ready, 1)

                def weigh(grp):
                    s = slice(grp * W8, (grp + 1) * W8)
                    got_ = got[grp % 2]
                    per_head = (NG + 1 - grp % 2) // 2
                    dve.wait_ge(gathered[grp % 2], g * (per_head * W8 * 16) + (grp // 2 + 1) * W8 * 16)
                    link(v.tensor_scalar(ti[:], top[:, s], -1.0, None, ALU.add))
                    link(v.tensor_scalar(tj[:], ti[:], TOP - 1, None, ALU.bitwise_and))
                    link(v.tensor_scalar(cnt[:], tj[:], 1.0, None, ALU.add))
                    link(v.tensor_scalar(r[:], top[:, s], ABSENT / 2, None, ALU.is_gt))
                    link(v.tensor_tensor(cnt[:], cnt[:], r[:], ALU.mult))
                    for q in range(GT):
                        c = slice(q * TOP, (q + 1) * TOP)
                        last = v.tensor_tensor_scan(incl[:, c], cnt[:, c], cnt[:, c], 0.0, ALU.bypass, ALU.add) if False else v.tensor_tensor_scan(
                            out=incl[:, c], data0=cnt[:, c], data1=cnt[:, c], initial=0.0, op0=ALU.add, op1=ALU.bypass)
                    link(last)
                    link(v.tensor_tensor(r[:], incl[:], cnt[:], ALU.subtract))
                    link(v.tensor_scalar(r[:], r[:], -1.0, float(TOP), ALU.mult, ALU.add))
                    link(v.scalar_tensor_tensor(out=take[:], in0=r[:], scalar=0.0, in1=cnt[:], op0=ALU.max, op1=ALU.min))
                    three = lambda x: x.rearrange("p (q i) -> p q i", i=TOP)
                    ai = keep["ai_flat"][:, bass.ds(g * NT + grp * GT, GT)].unsqueeze(2).broadcast_to([P, GT, TOP])
                    link(v.tensor_tensor(three(z[:]), three(got_[:, :, HC]), ai, ALU.add))
                    link(v.scalar_tensor_tensor(out=r[:], in0=z[:], scalar=0.2, in1=z[:], op0=ALU.mult, op1=ALU.max))
                    link(v.tensor_tensor(three(e[:]), three(r[:]), three(r[:])[:, :, 0:1].broadcast_to([P, GT, TOP]), ALU.subtract))
                    v.tensor_scalar(e[:], e[:], 0.0, None, ALU.min).then_inc(z_ready, 1)

                def mix(grp):
                    got_ = got[grp % 2]
                    three = lambda x: x.rearrange("p (q i) -> p q i", i=TOP)
                    dve.wait_ge(e_ready, g * NG + grp + 2)
                    link(v.tensor_tensor(e[:], e[:], take[:], ALU.mult))
                    link(v.tensor_reduce(den[:, 0, :], three(e[:]), AX.X, ALU.add))
                    link(v.reciprocal(den[:, 1, :], den[:, 0, :]))
                    link(v.tensor_tensor(three(e[:]), three(e[:]), den[:, 1, :].unsqueeze(2).broadcast_to([P, GT, TOP]), ALU.mult))
                    link(v.tensor_tensor(got_[:, :, 0:HC], got_[:, :, 0:HC], e[:].unsqueeze(2).broadcast_to([P, W8, HC]), ALU.mult))
                    dve.wait_ge(o_stored, g * (NG * 16) + grp * 16 + 16)
                    link(v.tensor_reduce(o[grp % 2][:], got_[:, :, 0:HC].rearrange("p (q i) c -> p q c i", i=TOP), AX.X, ALU.add))
                    dve.sem_inc(o_ready, 1)
                    dve.sem_inc(mixed, 1)

                for u in range(NT):
                    s = slice(u * TOP, (u + 1) * TOP)
                    dve.wait_ge(key_out, g * (NT * Q) + (u + 1) * Q + Q)
                    dve.sem_inc(tick, 1)
                    link(v.max(out=top[:, s], in_=key[u % 2][:]))
                    dve.sem_inc(tick, 1)
                    v.max_index(out=found[:, s], in_max=top[:, s], in_values=key[u % 2][:]).then_inc(picked, 1)
                    dve.wait_ge(picked, g * NT + u + 3)
                    v.tensor_scalar(index[:, s], found[:, s], head_base[:, bass.ds(g, 1)], None, ALU.add).then_inc(idx_ready, 1)
                    for grp in range(NG):
                        if u == min(GT * grp + 6, NT - 1):
                            weigh(grp)
                        if u == min(GT * grp + 7, NT - 1):
                            mix(grp)
                assert link.n == CHAIN, (link.n, CHAIN)


def finish(nc, t, a, out):
    with ExitStack() as ctx:
        sb = lambda n, s, d: ctx.enter_context(nc.sbuf_tensor("Z_" + n, s, d))
        sem = lambda n: ctx.enter_context(nc.semaphore("Z_" + n))
        x, y, e = sb("x", [P, NT, D], F32), sb("y", [P, NT, D], F32), sb("e", [P, NT, D], F32)
        loads, low, e_ready, chain, ready, stored = (sem(n) for n in ("loads", "low", "e_ready", "chain", "ready", "stored"))
        block = ctx.enter_context(nc.Block())

        @block.sync
        def _(sp):
            sp.dma_start(y[:], rows(t["y"])).then_inc(loads, 16)
            sp.dma_start(x[:], rows(t["x"])).then_inc(loads, 16)
            sp.wait_ge(ready, 1)
            sp.dma_start(rows(out), x[:]).then_inc(stored, 16)
            sp.wait_ge(stored, 16)

        @block.scalar
        def _(act):
            act.wait_ge(low, 1)
            nc.scalar.activation(e[:], e[:], ACT.Exp).then_inc(e_ready, 1)

        @block.vector
        def _(dve):
            link = Serial(dve, chain)
            dve.wait_ge(loads, 32)
            nc.vector.tensor_scalar(e[:], y[:], 0.0, None, ALU.min).then_inc(low, 1)
            link(nc.vector.tensor_scalar(y[:], y[:], 0.0, -1.0, ALU.max, ALU.add))
            link(nc.vector.tensor_tensor(x[:], x[:], y[:], ALU.add))
            dve.wait_ge(e_ready, 1)
            nc.vector.tensor_tensor(x[:], x[:], e[:], ALU.add).then_inc(ready, 1)


def clear_semaphores(nc):
    ended = sorted(set(nc.released_uncleared_semaphores))
    assert ended == list(range(ended[0], ended[-1] + 1))
    with nc.Block() as block:
        @block.gpsimd
        def _(pool):
            nc.gpsimd.sem_clear(range(ended[0], ended[-1] + 1))


def program(nc, a, out):
    dram = lambda n, s, d: nc.dram_tensor(n, s, d, kind="Internal").ap()
    t = {
        "P": dram("P_rows", (N, D), F32), "Q": dram("Q_rows", (N, D), F32), "C": dram("counts", (N, N), F16),
        "x": dram("x_rows", (N, D), F32), "h": dram("h_rows", (N, D), F32), "y": dram("y_rows", (N, D), F32),
        "ext": dram("edge_sums", (EXT, N), F32), "tab": dram("head_rows", (HEADS * N, RW), F32),
    }
    with ExitStack() as ctx:
        sb = lambda n, s, d: ctx.enter_context(nc.sbuf_tensor(n, s, d))
        keep = {
            "ident32": sb("ident32", [P, P], F32), "ident16": sb("ident16", [P, P], F16),
        }
        with ExitStack() as early:
            se = lambda n, s, d: early.enter_context(nc.sbuf_tensor(n, s, d))
            keep.update({
                "ident128": se("ident128", [128, 128], F32), "iota_d": se("iota_d", [128, 128], F16), "rowid": se("rowid", [128, 1], F32),
                "iota_s": se("iota_s", [P, N], F16), "chunk_of": se("chunk_of", [1, STEPS], I32), "window_of": se("window_of", [1, STEPS], I32),
                "base": se("base", [P, STEPS], F32), "same": se("same", [P, STEPS], F32),
                "G": se("G", [P, NT * MW], F32), "x": se("x_tile", [P, NT, D], F32), "h": se("h_tile", [P, NT, D], F32),
            })
            prepare(nc, t, a, keep)
            edge_loop(nc, t, a, keep)
            node_update(nc, t, a, keep)
        keep["CT"] = sb("counts_T", [P, NT * N], F16)
        turn_counts(nc, t, keep)
        sage(nc, t, a, keep)
        residual(nc, t, a, keep, "R1")
        clear_semaphores(nc)
        with ExitStack() as mid:
            keep["ha"] = mid.enter_context(nc.sbuf_tensor("ha", [P, NT, D + 1], F32))
            keep["a_col"] = mid.enter_context(nc.sbuf_tensor("a_col", [P, 2, NT], F32))
            project_in(nc, t, a, keep)
            attend(nc, t, a, keep, "E2")
            between(nc, t, a, keep)
            attend(nc, t, a, keep, "E4")
        residual(nc, t, a, keep, "R2", bias="b2")
        keep["ai_flat"] = sb("ai", [P, HEADS * NT], F32)
        keep["ai"] = keep["ai_flat"][:].rearrange("p (g j) -> p g j", j=NT)
        keep["aj"] = sb("aj", [P, HEADS, NT], F32)
        keep["rank"] = sb("rank", [P, 2, HEADS * NT], F32)
        project_heads(nc, t, a, keep)
        rank(nc, t, a, keep)
        top_attention(nc, t, a, keep)
    finish(nc, t, a, out)


_NAMES = {"x": "x", "src": "src", "dst": "dst", "edge_attr_16": "attr16", "edge_attr_3": "attr3"}
_NAMES.update({f"L0_gnn_{n}": n for n in ("W_msg1", "b_msg1", "W_msg2", "b_msg2", "W_gate", "b_gate", "W_upd1", "b_upd1", "W_upd2", "b_upd2", "ln_gamma", "ln_beta")})
_NAMES.update({"L1_gnn_Ws": "Ws", "L1_gnn_bs": "bs", "L1_gnn_ews": "ewsT", "L1_gnn_ebs": "ebs"})
_NAMES.update({f"L2_gnn_{n}": n for n in ("W1", "a1_src", "a1_dst", "b1", "W2", "a2_src", "a2_dst", "b2")})
_NAMES.update({"L3_gnn_W": "W3", "L3_gnn_att": "att"})


def kernel(**inputs):
    import numpy as _np
    import concourse.bacc as _bacc
    from concourse import mybir as _mybir
    from concourse.bass_utils import run_bass_kernel_spmd as _run

    nc = _bacc.Bacc("TRN2", target_bir_lowering=False, num_devices=1)
    arrays, args = {}, {}

    def put(name, short, v):
        v = _np.ascontiguousarray(v)
        arrays[name] = v
        args[short] = nc.dram_tensor(name, v.shape, _mybir.dt.from_np(v.dtype), kind="ExternalInput").ap()

    for name, short in _NAMES.items():
        v = _np.asarray(inputs[name])
        if short == "attr3":
            v = v.reshape(NC, P, ET, 3).transpose(0, 3, 2, 1)
        if short == "ewsT":
            v = v.transpose(0, 2, 1)
        put(f"in_{name}", short, v)
        if short in ("W1", "W2", "W3"):
            put(f"in_{name}_T", short + "T", v.T)
    out = nc.dram_tensor("out_x", (N, D), _mybir.dt.float32, kind="ExternalOutput").ap()
    program(nc, args, out)
    r = _run(nc, [arrays], core_ids=[0])
    return r.results[0]["out_x"]
```
